# Optimizing a Trainium2 kernel written in Bass

```python
import numpy as np
import jax
import jax.numpy as jnp

def _softmax(x, axis=-1):
    return jax.nn.softmax(x, axis=axis)

def _gelu(x):
    return jax.nn.gelu(x, approximate=True)

def _silu(x):
    return jax.nn.silu(x)

def _sigmoid(x):
    return jax.nn.sigmoid(x)

def _layernorm(x, axis=-1, eps=1e-05):
    m = jnp.mean(x, axis=axis, keepdims=True)
    v = jnp.var(x, axis=axis, keepdims=True)
    return (x - m) / jnp.sqrt(v + eps)

def _scatter_add(tgt, idx, src, axis=0):
    return tgt.at[idx].add(src)

def _segment_sum(src, seg, n):
    return jax.ops.segment_sum(src, seg, n)
kernel_name = 'mk_gnn_preln_d4_gnn_r8_3c9b1d'

def setup_inputs(seed: int=0):
    np.random.seed(seed)
    _w = jnp.asarray

    def _rec_inputs():
        import jax
        import jax.numpy as jnp
        _gk = jax.random.key(seed)
        x = -0.0003713 + 1 * jax.random.normal(jax.random.fold_in(_gk, 1), (6250, 128), jnp.float32)
        src = jax.random.randint(jax.random.fold_in(_gk, 2), (100000,), 0, 6250, jnp.int32)
        dst = jax.random.randint(jax.random.fold_in(_gk, 3), (100000,), 0, 6250, jnp.int32)
        _o = jnp.argsort(dst, stable=True)
        src = src[_o]
        dst = dst[_o]
        edge_type_2 = jax.random.randint(jax.random.fold_in(_gk, 12), (100000,), 0, 2, jnp.int32)
        edge_weight1 = jax.random.uniform(jax.random.fold_in(_gk, 13), (100000, 1), jnp.float32, 0.0, 1)
        return (x, src, dst, edge_type_2, edge_weight1)
    x, src, dst, edge_type_2, edge_weight1 = _rec_inputs()

    def _L0_gnn_setup():
        import jax, jax.numpy as jnp
        import numpy as np
        N_NODES = 12500
        N_EDGES = 200000
        NODE_DIM = 128
        HIDDEN = 128
        N_LAYERS = 4
        LN_EPS = 1e-05

        def _layernorm(x, g, b):
            mu = jnp.mean(x, axis=-1, keepdims=True)
            var = jnp.mean(jnp.square(x - mu), axis=-1, keepdims=True)
            return (x - mu) * jax.lax.rsqrt(var + LN_EPS) * g + b
        key = jax.random.key(seed)
        ks = jax.random.split(key, 16)
        s = 1.0 / np.sqrt(HIDDEN)
        inp = {'x': jax.random.normal(ks[0], (N_NODES, NODE_DIM), dtype=jnp.float32), 'edge_index': jax.random.randint(ks[1], (2, N_EDGES), 0, N_NODES, dtype=jnp.int64), 'Wn': jax.random.normal(ks[2], (NODE_DIM, HIDDEN), dtype=jnp.float32) / np.sqrt(NODE_DIM), 'bn': jnp.zeros((HIDDEN,), dtype=jnp.float32), 'WQ': jax.random.normal(ks[3], (N_LAYERS, HIDDEN, HIDDEN), dtype=jnp.float32) * s, 'bQ': jnp.zeros((N_LAYERS, HIDDEN), dtype=jnp.float32), 'WK': jax.random.normal(ks[4], (N_LAYERS, HIDDEN, HIDDEN), dtype=jnp.float32) * s, 'bK': jnp.zeros((N_LAYERS, HIDDEN), dtype=jnp.float32), 'WV': jax.random.normal(ks[5], (N_LAYERS, HIDDEN, HIDDEN), dtype=jnp.float32) * s, 'bV': jnp.zeros((N_LAYERS, HIDDEN), dtype=jnp.float32), 'WO': jax.random.normal(ks[6], (N_LAYERS, HIDDEN, HIDDEN), dtype=jnp.float32) * s, 'bO': jnp.zeros((N_LAYERS, HIDDEN), dtype=jnp.float32), 'ln_g': jnp.ones((N_LAYERS, HIDDEN), dtype=jnp.float32), 'ln_b': jnp.zeros((N_LAYERS, HIDDEN), dtype=jnp.float32), 'Wout': jax.random.normal(ks[7], (HIDDEN, NODE_DIM), dtype=jnp.float32) * s, 'bout': jnp.zeros((NODE_DIM,), dtype=jnp.float32)}
        return inp
    _L0_gnn_all = _L0_gnn_setup()
    _L0_gnn_in = {k: v for k, v in _L0_gnn_all.items() if k in ('Wn', 'bn', 'WQ', 'bQ', 'WK', 'bK', 'WV', 'bV', 'WO', 'bO', 'ln_g', 'ln_b', 'Wout', 'bout')}
    del _L0_gnn_all

    def _L1_gnn_setup():
        import jax, jax.numpy as jnp
        import numpy as np
        N, E, C, H = (12500, 75000, 128, 8)
        D = C // H
        REL_EDGE_TYPE = (1, 0)
        key = jax.random.key(seed)
        ks = jax.random.split(key, 16)
        s = 1.0 / np.sqrt(C)
        sd = 1.0 / np.sqrt(D)
        return {'x': jax.random.normal(ks[0], (N, C), jnp.float32), 'edge_index': jax.random.randint(ks[1], (2, E), 0, N), 'edge_type': jax.random.randint(ks[2], (E,), 0, 2), 'Wk': jax.random.normal(ks[3], (C, C), jnp.float32) * s, 'bk': jnp.zeros((C,), jnp.float32), 'Wq': jax.random.normal(ks[4], (C, C), jnp.float32) * s, 'bq': jnp.zeros((C,), jnp.float32), 'Wv': jax.random.normal(ks[5], (C, C), jnp.float32) * s, 'bv': jnp.zeros((C,), jnp.float32), 'a_rel': jax.random.normal(ks[6], (2, H, D, D), jnp.float32) * sd, 'm_rel': jax.random.normal(ks[7], (2, H, D, D), jnp.float32) * sd, 'p_rel': jnp.ones((2, H), jnp.float32), 'Wa': jax.random.normal(ks[8], (C, C), jnp.float32) * s, 'ba': jnp.zeros((C,), jnp.float32), 'skip': jnp.zeros((), jnp.float32)}
    _L1_gnn_all = _L1_gnn_setup()
    _L1_gnn_in = {k: v for k, v in _L1_gnn_all.items() if k in ('Wk', 'bk', 'Wq', 'bq', 'Wv', 'bv', 'a_rel', 'm_rel', 'p_rel', 'Wa', 'ba', 'skip')}
    del _L1_gnn_all

    def _L2_gnn_setup():
        import jax, jax.numpy as jnp
        import numpy as np
        N_NODES = 12500
        N_EDGES = 78125
        D_FEAT = 128
        OUT_DIM = 128
        key = jax.random.key(seed)
        k1, k2, k3, k4 = jax.random.split(key, 4)
        feature = jax.random.normal(k1, (N_NODES, D_FEAT), dtype=jnp.float32)
        relation_weight = jax.random.uniform(k2, (N_EDGES, 1), dtype=jnp.float32)
        relation_indices = jax.random.randint(k3, (2, N_EDGES), 0, N_NODES, dtype=jnp.int32)
        W = jax.random.normal(k4, (2 * D_FEAT, OUT_DIM), dtype=jnp.float32) * 0.05
        b = jnp.zeros((OUT_DIM,), dtype=jnp.float32)
        return {'feature': feature, 'relation_weight': relation_weight, 'W': W, 'b': b, 'relation_indices': relation_indices}
    _L2_gnn_all = _L2_gnn_setup()
    _L2_gnn_in = {k: v for k, v in _L2_gnn_all.items() if k in ('W', 'b')}
    del _L2_gnn_all

    def _L3_gnn_setup():
        import jax, jax.numpy as jnp
        import numpy as np
        N_NODES = 6250
        N_EDGES = 75000
        IN_CH = 128
        OUT_CH = 128
        key = jax.random.key(seed)
        k1, k2, k3, k4 = jax.random.split(key, 4)
        x = jax.random.normal(k1, (N_NODES, IN_CH), dtype=jnp.float32)
        edge_index = jax.random.randint(k2, (2, N_EDGES), 0, N_NODES, dtype=jnp.int64)
        W = jax.random.normal(k3, (OUT_CH, IN_CH), dtype=jnp.float32) * (1.0 / np.sqrt(IN_CH))
        b = jax.random.normal(k4, (OUT_CH,), dtype=jnp.float32) * 0.01
        return {'x': x, 'edge_index': edge_index, 'W': W, 'b': b}
    _L3_gnn_all = _L3_gnn_setup()
    _L3_gnn_in = {k: v for k, v in _L3_gnn_all.items() if k in ('W', 'b')}
    del _L3_gnn_all
    return {'x': x, 'src': src, 'dst': dst, 'edge_type_2': edge_type_2, 'edge_weight1': edge_weight1, 'L0_gnn_Wn': _L0_gnn_in['Wn'], 'L0_gnn_bn': _L0_gnn_in['bn'], 'L0_gnn_WQ': _L0_gnn_in['WQ'], 'L0_gnn_bQ': _L0_gnn_in['bQ'], 'L0_gnn_WK': _L0_gnn_in['WK'], 'L0_gnn_bK': _L0_gnn_in['bK'], 'L0_gnn_WV': _L0_gnn_in['WV'], 'L0_gnn_bV': _L0_gnn_in['bV'], 'L0_gnn_WO': _L0_gnn_in['WO'], 'L0_gnn_bO': _L0_gnn_in['bO'], 'L0_gnn_ln_g': _L0_gnn_in['ln_g'], 'L0_gnn_ln_b': _L0_gnn_in['ln_b'], 'L0_gnn_Wout': _L0_gnn_in['Wout'], 'L0_gnn_bout': _L0_gnn_in['bout'], 'L1_gnn_Wk': _L1_gnn_in['Wk'], 'L1_gnn_bk': _L1_gnn_in['bk'], 'L1_gnn_Wq': _L1_gnn_in['Wq'], 'L1_gnn_bq': _L1_gnn_in['bq'], 'L1_gnn_Wv': _L1_gnn_in['Wv'], 'L1_gnn_bv': _L1_gnn_in['bv'], 'L1_gnn_a_rel': _L1_gnn_in['a_rel'], 'L1_gnn_m_rel': _L1_gnn_in['m_rel'], 'L1_gnn_p_rel': _L1_gnn_in['p_rel'], 'L1_gnn_Wa': _L1_gnn_in['Wa'], 'L1_gnn_ba': _L1_gnn_in['ba'], 'L1_gnn_skip': _L1_gnn_in['skip'], 'L2_gnn_W': _L2_gnn_in['W'], 'L2_gnn_b': _L2_gnn_in['b'], 'L3_gnn_W': _L3_gnn_in['W'], 'L3_gnn_b': _L3_gnn_in['b']}

def reference(x, src, dst, edge_type_2, edge_weight1, L0_gnn_Wn, L0_gnn_bn, L0_gnn_WQ, L0_gnn_bQ, L0_gnn_WK, L0_gnn_bK, L0_gnn_WV, L0_gnn_bV, L0_gnn_WO, L0_gnn_bO, L0_gnn_ln_g, L0_gnn_ln_b, L0_gnn_Wout, L0_gnn_bout, L1_gnn_Wk, L1_gnn_bk, L1_gnn_Wq, L1_gnn_bq, L1_gnn_Wv, L1_gnn_bv, L1_gnn_a_rel, L1_gnn_m_rel, L1_gnn_p_rel, L1_gnn_Wa, L1_gnn_ba, L1_gnn_skip, L2_gnn_W, L2_gnn_b, L3_gnn_W, L3_gnn_b):
    import jax
    import jax.numpy as jnp

    def _L0_gnn_ref(x, edge_index, Wn, bn, WQ, bQ, WK, bK, WV, bV, WO, bO, ln_g, ln_b, Wout, bout):
        import jax, jax.numpy as jnp
        import numpy as np
        N_NODES = 12500
        N_EDGES = 200000
        NODE_DIM = 128
        HIDDEN = 128
        N_LAYERS = 4
        LN_EPS = 1e-05

        def _layernorm(x, g, b):
            mu = jnp.mean(x, axis=-1, keepdims=True)
            var = jnp.mean(jnp.square(x - mu), axis=-1, keepdims=True)
            return (x - mu) * jax.lax.rsqrt(var + LN_EPS) * g + b
        n = x.shape[0]
        src, dst = (edge_index[0], edge_index[1])
        scale = 1.0 / np.sqrt(HIDDEN)
        h = x @ Wn + bn
        for l in range(N_LAYERS):
            Q = h @ WQ[l] + bQ[l]
            K = h @ WK[l] + bK[l]
            V = h @ WV[l] + bV[l]
            scores = jnp.sum(Q[dst] * K[src], axis=-1) * scale
            seg_max = jax.ops.segment_max(scores, dst, num_segments=n)
            e = jnp.exp(scores - seg_max[dst])
            seg_sum = jax.ops.segment_sum(e, dst, num_segments=n)
            attn = e / seg_sum[dst]
            messages = jax.ops.segment_sum(attn[:, None] * V[src], dst, num_segments=n)
            out = messages @ WO[l] + bO[l]
            h = _layernorm(h + out, ln_g[l], ln_b[l])
        return h @ Wout + bout

    def _L1_gnn_ref(x, edge_index, edge_type, Wk, bk, Wq, bq, Wv, bv, a_rel, m_rel, p_rel, Wa, ba, skip):
        import jax, jax.numpy as jnp
        import numpy as np
        N, E, C, H = (12500, 75000, 128, 8)
        D = C // H
        REL_EDGE_TYPE = (1, 0)
        n = x.shape[0]
        k = (x @ Wk + bk).reshape(n, H, D)
        q = (x @ Wq + bq).reshape(n, H, D)
        v = (x @ Wv + bv).reshape(n, H, D)
        src, dst = (edge_index[0], edge_index[1])
        q_dst = q[dst]
        scale = 1.0 / jnp.sqrt(jnp.asarray(D, x.dtype))
        out = jnp.zeros((n, H, D), x.dtype)
        for r in range(2):
            mask = edge_type == REL_EDGE_TYPE[r]
            k_r = jnp.einsum('nhd,hde->nhe', k, a_rel[r])
            v_r = jnp.einsum('nhd,hde->nhe', v, m_rel[r])
            score = jnp.sum(q_dst * k_r[src], axis=-1) * p_rel[r] * scale
            score = jnp.where(mask[:, None], score, -jnp.inf)
            m = jax.ops.segment_max(score, dst, num_segments=n)
            m = jnp.where(jnp.isfinite(m), m, 0.0)
            e = jnp.where(mask[:, None], jnp.exp(score - m[dst]), 0.0)
            den = jax.ops.segment_sum(e, dst, num_segments=n)
            alpha = e / jnp.where(den[dst] > 0, den[dst], 1.0)
            msg = v_r[src] * alpha[..., None]
            out = out + jax.ops.segment_sum(msg, dst, num_segments=n)
        out = out.reshape(n, C)
        out = jax.nn.gelu(out, approximate=False) @ Wa + ba
        a = jax.nn.sigmoid(skip)
        return a * out + (1.0 - a) * x

    def _L2_gnn_ref(feature, relation_weight, W, b, relation_indices):
        import jax, jax.numpy as jnp
        import numpy as np
        N_NODES = 12500
        N_EDGES = 78125
        D_FEAT = 128
        OUT_DIM = 128
        dst = relation_indices[0]
        src = relation_indices[1]
        n = feature.shape[0]
        feat_n = feature[src] * relation_weight
        seg_sum = jax.ops.segment_sum(feat_n, dst, num_segments=n)
        seg_cnt = jax.ops.segment_sum(jnp.ones((src.shape[0], 1), feat_n.dtype), dst, num_segments=n)
        neigh_mean = seg_sum / jnp.maximum(seg_cnt, 1.0)
        h = jnp.concatenate([feature, neigh_mean], axis=-1)
        return h @ W + b

    def _L3_gnn_ref(x, edge_index, W, b):
        import jax, jax.numpy as jnp
        import numpy as np
        N_NODES = 6250
        N_EDGES = 75000
        IN_CH = 128
        OUT_CH = 128
        row, col = (edge_index[0], edge_index[1])
        n = x.shape[0]
        deg = jax.ops.segment_sum(jnp.ones_like(row, dtype=x.dtype), row, num_segments=n)
        deg_inv_sqrt = jnp.where(deg > 0, jax.lax.rsqrt(jnp.where(deg > 0, deg, 1.0)), 0.0)
        norm = deg_inv_sqrt[row] * deg_inv_sqrt[col]
        msgs = norm[:, None] * x[col]
        agg = jax.ops.segment_sum(msgs, row, num_segments=n)
        return agg @ W.T + b
    edge_index = jnp.stack([src, dst])
    h = jnp.maximum(_layernorm(x, axis=-1), 0.0)
    x = x + _L0_gnn_ref(h, edge_index, L0_gnn_Wn, L0_gnn_bn, L0_gnn_WQ, L0_gnn_bQ, L0_gnn_WK, L0_gnn_bK, L0_gnn_WV, L0_gnn_bV, L0_gnn_WO, L0_gnn_bO, L0_gnn_ln_g, L0_gnn_ln_b, L0_gnn_Wout, L0_gnn_bout)
    h = jnp.maximum(_layernorm(x, axis=-1), 0.0)
    x = x + _L1_gnn_ref(h, edge_index, edge_type_2, L1_gnn_Wk, L1_gnn_bk, L1_gnn_Wq, L1_gnn_bq, L1_gnn_Wv, L1_gnn_bv, L1_gnn_a_rel, L1_gnn_m_rel, L1_gnn_p_rel, L1_gnn_Wa, L1_gnn_ba, L1_gnn_skip)
    h = jnp.maximum(_layernorm(x, axis=-1), 0.0)
    x = x + _L2_gnn_ref(h, edge_weight1, L2_gnn_W, L2_gnn_b, edge_index)
    h = jnp.maximum(_layernorm(x, axis=-1), 0.0)
    x = x + _L3_gnn_ref(h, edge_index, L3_gnn_W, L3_gnn_b)
    return x

_drawn_inputs = setup_inputs


def setup_inputs(seed=0):
    import zlib

    import numpy as np

    out = dict(_drawn_inputs(seed))
    spreads = {'L0_gnn_bn': (0.0, 0.1),
     'L0_gnn_bQ': (0.0, 0.8),
     'L0_gnn_bK': (0.0, 0.8),
     'L0_gnn_bV': (0.0, 0.1),
     'L0_gnn_bO': (0.0, 0.1),
     'L0_gnn_ln_g': (1.0, 0.2),
     'L0_gnn_ln_b': (0.0, 0.1),
     'L0_gnn_bout': (0.0, 0.1),
     'L1_gnn_bk': (0.0, 0.8),
     'L1_gnn_bq': (0.0, 0.8),
     'L1_gnn_bv': (0.0, 0.308),
     'L1_gnn_p_rel': (1.0, 0.6),
     'L1_gnn_ba': (0.0, 0.298),
     'L2_gnn_b': (0.0, 0.1)}
    factors = {'edge_weight1': 3.517,
     'L1_gnn_Wk': 4.636,
     'L1_gnn_Wq': 4.502,
     'L1_gnn_a_rel': 4.501,
     'L3_gnn_b': 8.0}
    for name, (base, spread) in spreads.items():
        noise = np.random.default_rng([zlib.crc32(name.encode()), seed]).standard_normal(out[name].shape)
        drawn = base * np.exp(spread * noise) if base else spread * noise
        out[name] = jnp.asarray(drawn.astype(out[name].dtype))
    for name, factor in factors.items():
        out[name] = (out[name] * factor).astype(out[name].dtype)
    return out
```

```python
from contextlib import ExitStack

import numpy as np
import concourse.bass as bass
from concourse import mybir

F32 = mybir.dt.float32
BF16 = mybir.dt.bfloat16
I32 = mybir.dt.int32
ALU = mybir.AluOpType
ACT = mybir.ActivationFunctionType
AX = mybir.AxisListType
RMAX = bass.bass_isa.ReduceOp.max

P = 128
N = 6250
E = 100000
T = -(-N // P)
NPAD = T * P
PAD_ROW = N
LAST = N - (T - 1) * P
CH = 8
NCH = -(-E // (P * 2 * CH)) * 2 * CH
ECOL = NCH + CH
EFULL = E // NCH
EREST = E - EFULL * NCH
J = 4
B = 4
S = J * B
D_HEAD = 16
NSLOT = E + T * (J - 1)
EPOCH = 512
NEP = -(-NSLOT // (2 * S * EPOCH))
NG = 2 * EPOCH * NEP
NBLK = NG * B // P
REC = 4
BIG = float(2.0 ** 100)
DEGCAP = 2000
SCHED = NEP + 2


def ds(a, n):
    return bass.ds(a, n)


class Bag:
    pass


class Steps:

    def __init__(self, engine, sem, first=0):
        self.engine, self.sem, self.first, self.n = engine, sem, first, 0

    def __call__(self, instruction):
        instruction.then_inc(self.sem, 1)
        self.n += 1
        return instruction

    def wait(self, back=0):
        self.engine.wait_ge(self.sem, self.first + (self.n - back))


def open_stage(nc, ctx, names):
    names = [*dict.fromkeys([*names, "passed"])]
    sems = {n: ctx.enter_context(nc.semaphore(fresh(nc, n))) for n in names}
    nums = [sem.num for sem in sems.values()]
    sems["all"] = range(min(nums), max(nums) + 1)
    return sems


def close_stage(nc, sems):
    nc.gpsimd.dma_reset(sems["all"])
    nc.all_engine_barrier(sems_to_clear=sems["all"])


def fresh(nc, name):
    return f"{name}_{nc.next_id()}"


def buf(nc, ctx, name, shape, dtype=F32):
    return ctx.enter_context(nc.sbuf_tensor(fresh(nc, name), shape, dtype))


def psum(nc, ctx, name, shape, dtype=F32):
    return ctx.enter_context(nc.psum_tensor(fresh(nc, name), shape, dtype))


def constants(nc, c, k):
    k.iota_lo = buf(nc, c, "iota_lo", [P, P], BF16)
    k.iota_hi = buf(nc, c, "iota_hi", [P, T], BF16)
    k.iota_t = buf(nc, c, "iota_t", [P, T])
    k.node = buf(nc, c, "node", [P, T])
    k.ident = buf(nc, c, "ident", [P, P])
    k.ident_bf = buf(nc, c, "ident_bf", [P, P], BF16)
    k.ones = buf(nc, c, "ones", [P, P])
    k.after = buf(nc, c, "after", [P, P])
    k.chsel = buf(nc, c, "chsel", [CH, CH, P])
    with ExitStack() as s:
        m = open_stage(nc, s, ["counted", "ones_set", "masked"])
        with nc.Block() as block:
            @block.gpsimd
            def _(pool):
                pool.iota(k.iota_lo[:], [[1, P]], base=0, channel_multiplier=0, allow_small_or_imprecise_dtypes=True)
                pool.iota(k.iota_hi[:], [[1, T]], base=0, channel_multiplier=0, allow_small_or_imprecise_dtypes=True)
                pool.iota(k.iota_t[:], [[1, T]], base=0, channel_multiplier=0, allow_small_or_imprecise_dtypes=True)
                pool.iota(k.node[:], [[P, T]], base=0, channel_multiplier=1, allow_small_or_imprecise_dtypes=True)
                pool.memset(k.ones[:], 1.0).then_inc(m["ones_set"], 1)
                pool.memset(k.chsel[:], 1.0).then_inc(m["ones_set"], 1)
                pool.wait_ge(m["ones_set"], 2)
                pool.affine_select(k.ident[:], k.ones[:], [[-1, P]], ALU.is_equal, 0.0, base=0, channel_multiplier=1)
                pool.affine_select(k.ident_bf[:], k.ones[:], [[-1, P]], ALU.is_equal, 0.0, base=0, channel_multiplier=1)
                pool.affine_select(k.after[:], k.ones[:], [[-1, P]], ALU.is_gt, 0.0, base=0, channel_multiplier=1)
                pool.affine_select(k.chsel[:], k.chsel[:], [[-1, CH], [0, P]], ALU.is_equal, 0.0, base=0,
                                   channel_multiplier=1)
        close_stage(nc, m)


def edge_layout(nc, c, k, src, dst, kind, weight):
    k.src_f = buf(nc, c, "src_f", [P, ECOL])
    k.dst_f = buf(nc, c, "dst_f", [P, ECOL])
    k.kind_f = buf(nc, c, "kind_f", [P, ECOL])
    k.weight_f = buf(nc, c, "weight_f", [P, ECOL])
    k.beyond = buf(nc, c, "beyond", [P, ECOL], I32)
    with ExitStack() as s:
        m = open_stage(nc, s, ["blank", "loaded", "converted"])
        raw = {n: buf(nc, s, f"{n}_raw", [P, ECOL], I32) for n in ("src", "dst", "kind")}

        def load(sp, out, array):
            sp.dma_start(out[0:EFULL, 0:NCH], array[0:EFULL * NCH].rearrange("(p c) -> p c", c=NCH)).then_inc(m["loaded"], 16)
            sp.dma_start(out[EFULL:EFULL + 1, 0:EREST], array[EFULL * NCH:E].rearrange("(p c) -> p c", p=1)).then_inc(m["loaded"], 16)

        with nc.Block() as block:
            @block.gpsimd
            def _(pool):
                for n in ("src", "dst", "kind"):
                    pool.memset(raw[n][:], -1).then_inc(m["blank"], 1)
                pool.memset(k.weight_f[:], 0.0).then_inc(m["blank"], 1)

            @block.sync
            def _(sp):
                sp.wait_ge(m["blank"], 4)
                load(sp, raw["src"], src)
                load(sp, raw["dst"], dst)
                load(sp, raw["kind"], kind)
                load(sp, k.weight_f, weight)

            @block.vector
            def _(dve):
                dve.wait_ge(m["loaded"], 8 * 16)
                dve.tensor_copy(k.src_f[:], raw["src"][:])
                dve.tensor_copy(k.dst_f[:], raw["dst"][:])
                dve.tensor_copy(k.kind_f[:], raw["kind"][:])
                dve.tensor_scalar(k.beyond[:], raw["src"][:], 0.0, float(2 ** 26), ALU.is_lt, ALU.mult)
        close_stage(nc, m)


def split_keys(nc, k, key_f):
    with ExitStack() as s:
        m = open_stage(nc, s, ["own"])
        ki = buf(nc, s, "key_i", [P, ECOL], I32)
        hi = buf(nc, s, "hi_i", [P, ECOL], I32)
        lo = buf(nc, s, "lo_i", [P, ECOL], I32)
        with nc.Block() as block:
            @block.vector
            def _(dve):
                own = Steps(dve, m["own"])
                own(dve.tensor_copy(ki[:], key_f[:]))
                own.wait()
                own(dve.tensor_scalar(hi[:], ki[:], 7, None, ALU.arith_shift_right))
                own.wait()
                own(dve.tensor_copy(k.hi[:], hi[:]))
                own(dve.tensor_scalar(lo[:], hi[:], float(-P), None, ALU.mult))
                own.wait()
                own(dve.tensor_tensor(k.lo[:], key_f[:], lo[:], ALU.add))
                own.wait()
        close_stage(nc, m)


def one_hots(dve, k, oh, col):
    dve.tensor_tensor(oh[:, :, 0:P], k.lo[:, ds(col, CH)].unsqueeze(2).to_broadcast([P, CH, P]),
                      k.iota_lo[:].unsqueeze(1).to_broadcast([P, CH, P]), ALU.is_equal)
    return dve.tensor_tensor(oh[:, :, P:P + T], k.hi[:, ds(col, CH)].unsqueeze(2).to_broadcast([P, CH, T]),
                             k.iota_hi[:].unsqueeze(1).to_broadcast([P, CH, T]), ALU.is_equal)


def histogram(nc, k, oh, deg):
    with ExitStack() as s:
        m = open_stage(nc, s, ["hot", "hot_used", "zeroed", "summed"])
        zero = buf(nc, s, "hist_zero", [P, P], BF16)
        count = psum(nc, s, "hist_count", [P, 512], F32)
        with nc.Block() as block:
            @block.vector
            def _(dve):
                dve.memset(zero[:], 0.0).then_inc(m["zeroed"], 1)
                dve.nop().then_inc(m["hot_used"], 2)
                with dve.Fori(0, NCH // (2 * CH)) as i:
                    for q in range(2):
                        dve.wait_ge(m["hot_used"], i * 2 + (q + 1))
                        one_hots(dve, k, oh[q], i * (2 * CH) + q * CH).then_inc(m["hot"], 1)
                dve.wait_ge(m["summed"], 1)
                dve.tensor_copy(deg[:], count[:, 0:T])

            @block.tensor
            def _(pe):
                pe.wait_ge(m["zeroed"], 1)
                pe.matmul(count[:, 0:T], zero[:], zero[:, 0:T], start=True, stop=True, skip_group_check=True)
                with pe.Fori(0, NCH // (2 * CH)) as i:
                    for q in range(2):
                        pe.wait_ge(m["hot"], i * 2 + (q + 1))
                        for c in range(CH):
                            mm = pe.matmul(count[:, 0:T], oh[q][:, c, 0:P], oh[q][:, c, P:P + T], start=False, stop=True,
                                           skip_group_check=True)
                        mm.then_inc(m["hot_used"], 1)
                pe.matmul(count[:, 0:T], zero[:], zero[:, 0:T], start=False, stop=True, skip_group_check=True).then_inc(m["summed"], 1)
        close_stage(nc, m)


TD = 22


def sort_by_degree(nc, k, deg, place, perm_d, keys_d, tmap_d, sched, perm, deg_p):
    with ExitStack() as s:
        m = open_stage(nc, s, ["own", "keys_ready", "keys_out", "keys_in", "ranked", "act_ranked", "slots", "slots_max",
                               "info", "scattered", "tmap_ready", "stored", "summed_ps"])
        keys = buf(nc, s, "keys", [P, T])
        nkeys = buf(nc, s, "nkeys", [P, T])
        row = buf(nc, s, "key_row", [P, NPAD])
        junk_v = buf(nc, s, "junk_v", [P, NPAD], BF16)
        junk_a = buf(nc, s, "junk_a", [P, NPAD], BF16)
        rank = buf(nc, s, "rank", [P, T])
        rank_i = buf(nc, s, "rank_i", [P, T], I32)
        ti = buf(nc, s, "ti", [P, T], I32)
        pi = buf(nc, s, "pi", [P, T], I32)
        tf = buf(nc, s, "tf", [P, T])
        pf = buf(nc, s, "pf", [P, T])
        mine = buf(nc, s, "mine", [P, T, T])
        part = buf(nc, s, "part", [P, T, T])
        smax = buf(nc, s, "smax", [P, T])
        sall = buf(nc, s, "sall", [P, T])
        nb_i = buf(nc, s, "nb_i", [P, T], I32)
        nb = buf(nc, s, "nb", [P, T])
        cum = buf(nc, s, "cum", [P, T])
        base = buf(nc, s, "base", [P, T])
        zeros = buf(nc, s, "zeros_t", [P, T])
        info = buf(nc, s, "info", [P, T, 2])
        got = buf(nc, s, "got", [P, T, 2])
        blk = buf(nc, s, "blk", [P, NBLK])
        tm = buf(nc, s, "tm", [P, NBLK])
        tm_i = buf(nc, s, "tm_i", [P, NBLK], I32)
        sc_f = buf(nc, s, "sc_f", [1, NEP + 1])
        sc_i = buf(nc, s, "sc_i", [1, 4], I32)
        ep0 = buf(nc, s, "ep0", [1, NEP])
        big = buf(nc, s, "tm_cmp", [P, NBLK // 4, T], BF16)
        with nc.Block() as block:
            @block.vector
            def _(dve):
                own = Steps(dve, m["own"])
                own(dve.tensor_scalar(keys[:], deg[:], float(DEGCAP), float(NPAD), ALU.min, ALU.mult))
                own(dve.memset(zeros[:], 0.0))
                own.wait()
                own(dve.tensor_tensor(keys[:], keys[:], k.node[:], ALU.subtract))
                own.wait()
                own(dve.tensor_scalar(keys[:], keys[:], float(NPAD - 1), None, ALU.add))
                own.wait()
                dve.tensor_scalar(nkeys[:], keys[:], -1.0, None, ALU.mult).then_inc(m["keys_ready"], 1)
                dve.wait_ge(m["keys_in"], 16)
                with dve.Fori(0, TD) as t:
                    dve.tensor_scalar(junk_v[:], row[:], keys[:, ds(t, 1)], None, ALU.is_gt, ALU.add,
                                      accum_out=rank[:, ds(t, 1)]).then_inc(m["ranked"], 1)
                    dve.wait_ge(m["ranked"], t + 1)
                dve.wait_ge(m["ranked"], TD)
                dve.wait_ge(m["act_ranked"], T - TD)
                own(dve.tensor_scalar(rank[:, TD:T], rank[:, TD:T], float(NPAD - 1), 0.5, ALU.add, ALU.mult))
                own.wait()
                own(dve.tensor_copy(rank_i[:], rank[:]))
                own.wait()
                own(dve.tensor_scalar(ti[:], rank_i[:], 7, None, ALU.arith_shift_right))
                own(dve.tensor_scalar(pi[:], rank_i[:], P - 1, None, ALU.bitwise_and))
                own(dve.tensor_copy(info[:, :, 0], k.node[:]))
                dve.tensor_copy(info[:, :, 1], deg[:]).then_inc(m["info"], 1)
                own.wait()
                own(dve.tensor_copy(tf[:], ti[:]))
                own(dve.tensor_copy(pf[:], pi[:]))
                own.wait()
                own(dve.tensor_tensor(mine[:], k.iota_t[:].unsqueeze(2).to_broadcast([P, T, T]),
                                      tf[:].unsqueeze(1).to_broadcast([P, T, T]), ALU.is_equal))
                own.wait()
                own(dve.tensor_tensor(part[:], mine[:], deg[:].unsqueeze(1).to_broadcast([P, T, T]), ALU.mult))
                own.wait()
                dve.tensor_reduce(smax[:], part[:], AX.X, ALU.max).then_inc(m["slots"], 1)
                dve.wait_ge(m["slots_max"], 1)
                own(dve.tensor_scalar(nb_i[:], sall[:], float(J - 1), None, ALU.add))
                own.wait()
                own(dve.tensor_scalar(nb_i[:], nb_i[:], int(np.log2(J)), None, ALU.arith_shift_right))
                own.wait()
                own(dve.tensor_copy(nb[:], nb_i[:]))
                own.wait()
                own(dve.tensor_tensor_scan(cum[:], nb[:], zeros[:], 0.0, ALU.add, ALU.add))
                own.wait()
                own(dve.tensor_tensor(base[:], cum[:], nb[:], ALU.subtract))
                own.wait()
                own(dve.tensor_scalar(base[:], base[:], float(J * P), None, ALU.mult))
                own.wait()
                own(dve.tensor_tensor(part[:], mine[:], base[:].unsqueeze(2).to_broadcast([P, T, T]), ALU.mult))
                own.wait()
                own(dve.tensor_reduce(place[:], part[:].rearrange("p t n -> p n t"), AX.X, ALU.add))
                own.wait()
                own(dve.tensor_tensor(place[:], place[:], pf[:], ALU.add))
                for r in range(4):
                    q = slice(r * (NBLK // 4), (r + 1) * (NBLK // 4))
                    own.wait()
                    own(dve.tensor_tensor(big[:], cum[:].unsqueeze(1).to_broadcast([P, NBLK // 4, T]),
                                          blk[:, q].unsqueeze(2).to_broadcast([P, NBLK // 4, T]), ALU.is_le))
                    own.wait()
                    own(dve.tensor_reduce(tm[:, q], big[:], AX.X, ALU.add))
                own.wait()
                dve.tensor_scalar(tm_i[:], tm[:], float(T - 1), None, ALU.min).then_inc(m["tmap_ready"], 1)
                own(dve.tensor_scalar(sc_i[:, 0:1], cum[0:1, T - 1:T], float(2 * B - 1), None, ALU.add))
                own.wait()
                own(dve.tensor_scalar(sc_i[:, 1:2], sc_i[:, 0:1], int(np.log2(2 * B)), None, ALU.arith_shift_right))
                own.wait()
                own(dve.tensor_scalar(sc_i[:, 2:3], sc_i[:, 1:2], float(EPOCH - 1), None, ALU.add))
                own(dve.tensor_copy(sc_f[:, NEP:NEP + 1], sc_i[:, 1:2]))
                own.wait()
                own(dve.tensor_scalar(sc_i[:, 3:4], sc_i[:, 2:3], int(np.log2(EPOCH)), None, ALU.arith_shift_right))
                own(dve.tensor_tensor(sc_f[:, 0:NEP], sc_f[:, NEP:NEP + 1].to_broadcast([1, NEP]), ep0[:], ALU.subtract))
                own.wait()
                own(dve.tensor_scalar(sc_f[:, 0:NEP], sc_f[:, 0:NEP], 1.0, float(EPOCH), ALU.max, ALU.min))
                own(dve.tensor_scalar(sched[:, NEP:NEP + 1], sc_i[:, 3:4], 1.0, None, ALU.max))
                own(dve.tensor_scalar(sched[:, NEP + 1:NEP + 2], sc_i[:, 1:2], 1.0, None, ALU.max))
                own.wait()
                own(dve.tensor_copy(sched[:, 0:NEP], sc_f[:, 0:NEP]))
                dve.wait_ge(m["stored"], 32)
                own(dve.tensor_copy(perm[:], got[:, :, 0]))
                own(dve.tensor_copy(deg_p[:], got[:, :, 1]))
                own.wait()

            @block.scalar
            def _(act):
                act.wait_ge(m["keys_in"], 16)
                with act.Fori(TD, T) as t:
                    act.activation(junk_a[:], row[:], ACT.Sign, bias=nkeys[:, ds(t, 1)],
                                   accum_out=rank[:, ds(t, 1)]).then_inc(m["act_ranked"], 1)
                    act.wait_ge(m["act_ranked"], t - (TD - 1))

            @block.gpsimd
            def _(pool):
                pool.iota(blk[:], [[1, NBLK]], base=0, channel_multiplier=NBLK, allow_small_or_imprecise_dtypes=True)
                pool.iota(ep0[:], [[EPOCH, NEP]], base=0, channel_multiplier=0, allow_small_or_imprecise_dtypes=True)
                pool.wait_ge(m["info"], 1)
                for t in range(T):
                    pool.indirect_dma_start(perm_d, bass.IndirectOffsetOnAxis(rank_i[:, t:t + 1], 0), info[:, t, :], None
                                            ).then_inc(m["scattered"], 16)
                pool.wait_ge(m["slots"], 1)
                pool.partition_all_reduce(sall[:], smax[:], P, RMAX).then_inc(m["slots_max"], 1)

            @block.sync
            def _(sp):
                sp.wait_ge(m["keys_ready"], 1)
                sp.dma_start(keys_d.rearrange("(h l) -> l h", l=P), keys[:], allow_slow_non_contiguous=True).then_inc(m["keys_out"], 16)
                sp.wait_ge(m["keys_out"], 16)
                sp.dma_start(row[:], keys_d.partition_broadcast(P)).then_inc(m["keys_in"], 16)
                sp.wait_ge(m["tmap_ready"], 1)
                sp.dma_start(tmap_d.rearrange("(p j) -> p j", p=P), tm_i[:]).then_inc(m["stored"], 16)
                sp.wait_ge(m["scattered"], 16 * T)
                sp.dma_start(got[:], perm_d.rearrange("(t p) c -> p t c", p=P)).then_inc(m["stored"], 16)
                sp.wait_ge(m["stored"], 32)
        close_stage(nc, m)


def prefill(nc, k, empty, ell_d, sched):
    with ExitStack() as s:
        m = open_stage(nc, s, ["written", "passed"])
        with nc.Block() as block:
            @block.sync
            def _(sp):
                epochs = sp.value_load(sched[0:1, NEP:NEP + 1], min_val=1, max_val=NEP)
                sp.dma_start(k.scrap_d[0], empty[:, 0, :]).then_inc(m["written"], 16)
                with sp.Fori(0, epochs) as e:
                    pairs = sp.value_load(sched[0:1, ds(e, 1)], min_val=1, max_val=EPOCH)
                    with sp.Fori(0, pairs) as i:
                        sp.wait_ge(m["written"], e * (EPOCH * 16) + (i * 16 + 16))
                        sp.dma_start(ell_d[ds(e * EPOCH + i, 1)].rearrange("a g p r -> p (a g) r"),
                                     empty[:].rearrange("p (g s) r -> p g (s r)", g=2)).then_inc(m["written"], 16)
                last = sp.value_load(sched[0:1, NEP + 1:NEP + 2], min_val=1, max_val=EPOCH * NEP)
                sp.wait_ge(m["written"], last * 16 + 16)
                sp.sem_inc(m["passed"], 1)
        close_stage(nc, m)


def place_edges(nc, k, key_f, oh, place, records, ell_d):
    G2 = 2 * CH
    with ExitStack() as s:
        m = open_stage(nc, s, ["own", "table_set", "zeroed", "hot", "keycol", "keysT_ps", "keysT_sb", "hotT_ps", "hotT_sb", "rows_ps",
                               "taken", "snapped", "counted", "addressed", "scat0", "scat1", "passed"])
        scat = [m["scat0"], m["scat1"]]
        zero = buf(nc, s, "build_zero", [P, P], BF16)
        table = [buf(nc, s, f"table{r}", [P, 2, T]) for r in range(2)]
        keycol = [buf(nc, s, f"keycol{q}", [P, CH]) for q in range(2)]
        keysT = buf(nc, s, "keysT", [CH, P])
        hotT = buf(nc, s, "hotT", [P, CH, P])
        junk = buf(nc, s, "rank_junk", [P, CH, P])
        rk = buf(nc, s, "rk", [P, CH])
        sel = buf(nc, s, "sel", [P, CH, 2, T])
        cp = buf(nc, s, "cp", [P, CH, 2])
        v = buf(nc, s, "v_f", [P, CH])
        vi = buf(nc, s, "v_i", [P, CH], I32)
        va = buf(nc, s, "v_a", [P, CH], I32)
        vb = buf(nc, s, "v_b", [P, CH], I32)
        vc = buf(nc, s, "v_c", [P, CH], I32)
        idx = [buf(nc, s, f"slot_idx{q}", [P, CH], I32) for q in range(2)]
        rec = [buf(nc, s, f"slot_rec{q}", [P, CH, REC]) for q in range(2)]
        warm = buf(nc, s, "warm", [P, REC])
        ps_kt = psum(nc, s, "ps_kt", [CH, 512], F32)
        ps_ht = psum(nc, s, "ps_ht", [P, CH, P], BF16)
        ps_row = psum(nc, s, "ps_row", [P, CH, P], F32)
        ps_find = psum(nc, s, "ps_find", [P, CH, P], F32)
        ps_cnt = psum(nc, s, "ps_cnt", [P, 512], F32)
        steps = NCH // G2
        with nc.Block() as block:
            @block.vector
            def _(dve):
                dve.memset(zero[:], 0.0).then_inc(m["zeroed"], 1)
                dve.memset(table[0][:, 0, :], 0.0).then_inc(m["snapped"], 1)
                dve.nop().then_inc(m["taken"], 1)
                dve.tensor_copy(table[0][:, 1, :], place[:]).then_inc(m["table_set"], 1)
                dve.tensor_copy(table[1][:, 1, :], place[:]).then_inc(m["table_set"], 1)
                dve.memset(warm[:], 0.0).then_inc(m["table_set"], 1)
                one_hots(dve, k, oh[0], 0).then_inc(m["hot"], 1)
                PER = CH + 9
                with dve.Fori(0, steps) as i:
                    for q in range(2):
                        g = i * 2 + q
                        own = Steps(dve, m["own"], i * (2 * PER) + q * PER)
                        one_hots(dve, k, oh[1 - q], (i * 2 + (q + 1)) * CH).then_inc(m["hot"], 1)
                        dve.wait_ge(m["rows_ps"], i * 2 + (q + 1))
                        for c in range(CH):
                            ins = dve.scalar_tensor_tensor(junk[:, c, :], ps_row[:, c, :], keycol[q][:, c:c + 1],
                                                           k.after[:], ALU.is_equal, ALU.mult, accum_out=rk[:, c:c + 1])
                            own(ins)
                        dve.wait_ge(m["counted"], i * G2 + (q + 1) * CH)
                        own(dve.tensor_tensor(sel[:], ps_find[:, :, 0:2 * T].rearrange("p c (a t) -> p c a t", a=2),
                                              oh[q][:, :, P:P + T].unsqueeze(2).to_broadcast([P, CH, 2, T]), ALU.mult))
                        own.wait()
                        own(dve.tensor_reduce(cp[:], sel[:], AX.X, ALU.add))
                        own.wait()
                        dve.nop().then_inc(m["taken"], 1)
                        own(dve.tensor_tensor(v[:], cp[:, :, 0], rk[:], ALU.add))
                        own.wait()
                        own(dve.scalar_tensor_tensor(vi[:], v[:], float(P), cp[:, :, 1], ALU.mult, ALU.add))
                        own.wait()
                        own(dve.tensor_scalar(va[:], vi[:], 11, 11, ALU.arith_shift_right, ALU.logical_shift_left))
                        own(dve.tensor_scalar(vb[:], vi[:], P - 1, 4, ALU.bitwise_and, ALU.logical_shift_left))
                        own(dve.tensor_scalar(vc[:], vi[:], 7, S - 1, ALU.arith_shift_right, ALU.bitwise_and))
                        own.wait()
                        own(dve.tensor_tensor(vc[:], vc[:], vb[:], ALU.bitwise_or))
                        own.wait()
                        own(dve.tensor_tensor(va[:], va[:], vc[:], ALU.bitwise_or))
                        assert own.n == PER
                        own.wait()
                        dve.wait_ge(scat[q], i * (CH * 16) + 16)
                        dve.tensor_tensor(idx[q][:], va[:], k.beyond[:, ds((i * 2 + q) * CH, CH)], ALU.bitwise_or)
                        dve.tensor_copy(rec[q][:], records[:, ds((i * 2 + q) * CH, CH), :]).then_inc(m["addressed"], 1)

            @block.tensor
            def _(pe):
                pe.wait_ge(m["zeroed"], 1)
                pe.wait_ge(m["table_set"], 3)
                pe.matmul(ps_cnt[:, 0:T], zero[:], zero[:, 0:T], start=True, stop=True, skip_group_check=True)
                with pe.Fori(0, steps) as i:
                    for q in range(2):
                        g = i * 2 + (q + 1)
                        pe.wait_ge(m["keycol"], g)
                        pe.transpose(ps_kt[:, 0:P], keycol[q][:], k.ident[:]).then_inc(m["keysT_ps"], 1)
                        pe.wait_ge(m["hot"], g)
                        for c in range(CH):
                            mm = pe.transpose(ps_ht[:, c, :], oh[q][:, c, 0:P], k.ident_bf[:])
                        mm.then_inc(m["hotT_ps"], 1)
                        pe.wait_ge(m["keysT_sb"], g)
                        pe.wait_ge(m["taken"], g)
                        for c in range(CH):
                            mm = pe.matmul(ps_row[:, c, :], k.chsel[:, c, :], keysT[:], start=True, stop=True)
                        mm.then_inc(m["rows_ps"], 1)
                        pe.wait_ge(m["hotT_sb"], g)
                        for c in range(CH):
                            pe.wait_ge(m["snapped"], i * G2 + (q * CH + c + 1))
                            pe.matmul(ps_find[:, c, 0:2 * T], hotT[:, c, :], table[c % 2][:], start=True, stop=True)
                            mm = pe.matmul(ps_cnt[:, 0:T], oh[q][:, c, 0:P], oh[q][:, c, P:P + T], start=False, stop=True,
                                           skip_group_check=True)
                            mm.then_inc(m["counted"], 1)

            @block.scalar
            def _(act):
                with act.Fori(0, steps) as i:
                    for q in range(2):
                        g = i * 2 + (q + 1)
                        act.copy(keycol[q][:], key_f[:, ds((i * 2 + q) * CH, CH)]).then_inc(m["keycol"], 1)
                        act.wait_ge(m["keysT_ps"], g)
                        act.copy(keysT[:], ps_kt[:, 0:P]).then_inc(m["keysT_sb"], 1)
                        act.wait_ge(m["hotT_ps"], g)
                        act.copy(hotT[:], ps_ht[:]).then_inc(m["hotT_sb"], 1)
                        for c in range(CH):
                            act.wait_ge(m["counted"], i * G2 + (q * CH + c + 1))
                            act.copy(table[(c + 1) % 2][:, 0, :], ps_cnt[:, 0:T]).then_inc(m["snapped"], 1)

            @block.gpsimd
            def _(pool):
                pool.wait_ge(m["table_set"], 3)
                for q in range(2):
                    pool.dma_start(k.scrap_d[q], warm[:]).then_inc(scat[q], 16)
                with pool.Fori(0, steps) as i:
                    for q in range(2):
                        pool.wait_ge(m["addressed"], i * 2 + (q + 1))
                        pool.sem_inc(m["passed"], 1)
                        for c in range(CH):
                            pool.indirect_dma_start(ell_d, bass.IndirectOffsetOnAxis(idx[q][:, c:c + 1], 0),
                                                    rec[q][:, c, :], None, bounds_check=NG * P * S - 1,
                                                    oob_is_err=False).then_inc(scat[q], 16)
                for q in range(2):
                    pool.wait_ge(scat[q], 16 + steps * CH * 16)
        close_stage(nc, m)


GPI = 2 * S
HALF = float(2.0 ** 98)


def edge_pass(nc, k, mode, table_d, table_rows, width, ell_d, tmap_d, sched):
    soft = mode in ("attend", "heads")
    R = 1 if mode == "attend" else 16
    W = {"attend": P + 1, "heads": R * (D_HEAD + 1), "weigh": P, "sum": P}[mode]
    PSW = 256 if W <= 256 else 512
    gw = {"attend": P + 1, "heads": 2 * P}.get(mode, P)
    with ExitStack() as s:
        m = open_stage(nc, s, ["own", "a_own", "listed0", "listed1", "numbered", "read0", "read1", "released0", "released1", "scored", "powered",
                               "weighted", "summed", "sum_taken", "passed", "dve_passed"]
                       + [f"got{q}{b}" for q in range(2) for b in range(B)])
        listed, released, read = [m["listed0"], m["listed1"]], [m["released0"], m["released1"]], [m["read0"], m["read1"]]
        got = [[m[f"got{q}{b}"] for b in range(B)] for q in range(2)]
        meta = [buf(nc, s, f"meta{q}", [P, S, REC]) for q in range(2)]
        tiles = [buf(nc, s, f"tiles{q}", [1, B], I32) for q in range(2)]
        idx = [buf(nc, s, f"row_idx{q}", [P, S], I32) for q in range(2)]
        rows = [buf(nc, s, f"rows{q}", [P, S, gw]) for q in range(2)]
        wide = buf(nc, s, "weighted_rows", [P, S, W]) if mode != "sum" else None
        if soft:
            prod = buf(nc, s, "prod", [P, S, gw if mode == "attend" else P])
            score = buf(nc, s, "score", [P, S, R])
            masks = buf(nc, s, "masks", [P, S, 2])
            nmb = buf(nc, s, "nmb", [P, B, R])
            nmo = buf(nc, s, "nmo", [P, B, R])
            nmn = buf(nc, s, "nmn", [P, B, R])
            expo = buf(nc, s, "expo", [P, S + B, R])
            corr = buf(nc, s, "corr", [P, S + B, R])
            kept = buf(nc, s, "kept", [P, W]) if mode == "heads" else None
        total = psum(nc, s, "ps_total", [P, B, PSW], F32)
        epochs = nc.values_load(sched[0:1, NEP:NEP + 1], min_val=1, max_val=NEP)
        with nc.Block() as block:
            @block.vector
            def _(dve):
                dve.memset(k.acc[:], 0.0)
                dve.memset(k.nm[:], HALF)
                if mode == "attend":
                    for q in range(2):
                        dve.memset(rows[q][:, :, P:P + 1], 1.0)
        with nc.Fori(0, epochs) as e:
            pairs = nc.values_load(sched[0:1, ds(e, 1)], min_val=1, max_val=EPOCH)
            with nc.Block() as block:
                @block.sync
                def _(sp):
                    with sp.Fori(0, pairs) as i:
                        for q in range(2):
                            g = e * (2 * EPOCH) + (i * 2 + q)
                            sp.wait_ge(read[q], i + 1)
                            sp.dma_start(meta[q][:].rearrange("p s r -> p (s r)"),
                                         ell_d[ds(g, 1)].rearrange("a p r -> (a p) r")).then_inc(listed[q], 16)
                            sp.dma_start(tiles[q][:], tmap_d[ds(g, 1), :]).then_inc(listed[q], 16)

                @block.gpsimd
                def _(pool):
                    with pool.Fori(0, pairs) as i:
                        for q in range(2):
                            pool.wait_ge(listed[q], i * 32 + 32)
                            pool.sem_inc(m["passed"], 1)
                            pool.tensor_copy(idx[q][:], meta[q][:, :, 1 if mode == "heads" else 0]).then_inc(m["numbered"], 1)
                            pool.wait_ge(m["numbered"], i * 2 + (q + 1))
                            pool.wait_ge(released[q], i + 1)
                            pool.sem_inc(m["passed"], 1)
                            for j in range(S):
                                pool.indirect_dma_start(rows[q][:, j, 0:width], None, table_d,
                                                        bass.IndirectOffsetOnAxis(idx[q][:, j:j + 1], 0)
                                                        ).then_inc(got[q][j // J], 16)

                @block.tensor
                def _(pe):
                    with pe.Fori(0, pairs) as i:
                        for q in range(2):
                            g1 = i * 2 + (q + 1)
                            pe.wait_ge(m["sum_taken"], g1)
                            if mode != "sum":
                                if mode == "heads":
                                    pe.wait_ge(m["weighted"], g1)
                            for b in range(B):
                                if mode == "sum":
                                    pe.wait_ge(got[q][b], i * (16 * J) + 16 * J)
                                elif mode != "heads":
                                    pe.wait_ge(m["weighted"], (i * 2 + q) * B + (b + 1))
                                for j in range(b * J, b * J + J):
                                    src = rows[q][:, j, :] if mode == "sum" else wide[:, j, :]
                                    mm = pe.matmul(total[:, b, 0:W], k.ident[:], src, start=(j == b * J),
                                                   stop=(j == b * J + J - 1))
                            mm.then_inc(m["summed"], 1)

                @block.scalar
                def _(act):
                    with act.Fori(0, pairs) as i:
                        for q in range(2):
                            g1 = i * 2 + (q + 1)
                            if mode == "attend":
                                act.wait_ge(m["scored"], g1)
                                act.activation(corr[:], expo[:], ACT.Exp).then_inc(m["powered"], 1)
                                act.wait_ge(m["powered"], g1)
                                act.wait_ge(m["summed"], g1)
                                for j in range(S):
                                    ins = act.activation(wide[:, j, :], rows[q][:, j, :], ACT.Copy, scale=corr[:, j, :])
                                    if j % J == J - 1:
                                        ins.then_inc(m["weighted"], 1)
                            if mode == "heads":
                                act.wait_ge(m["scored"], g1)
                                act.wait_ge(m["summed"], g1)
                                act.activation(wide[:].rearrange("p s (r d) -> p s r d", d=D_HEAD + 1)[:, :, :, D_HEAD],
                                               expo[:, 0:S, :], ACT.Exp).then_inc(m["powered"], 1)
                                act.activation(corr[:, S:S + B, :], expo[:, S:S + B, :], ACT.Exp).then_inc(m["powered"], 1)
                            if mode == "weigh":
                                act.wait_ge(m["summed"], g1)
                                for j in range(S):
                                    if j % J == 0:
                                        act.wait_ge(got[q][j // J], i * (16 * J) + 16 * J)
                                    ins = act.activation(wide[:, j, :], rows[q][:, j, :], ACT.Copy,
                                                         scale=meta[q][:, j, 3:4])
                                    if j % J == J - 1:
                                        ins.then_inc(m["weighted"], 1)

                @block.vector
                def _(dve):
                    dve.nop().then_inc(released[0], 1)
                    dve.nop().then_inc(released[1], 1)
                    dve.nop().then_inc(read[0], 1)
                    dve.nop().then_inc(read[1], 1)
                    dve.nop().then_inc(m["sum_taken"], 1)
                    dve.nop().then_inc(m["summed"], 1)
                    PER = {"attend": 2 * B + 2 + 2 * B + 4 + B, "heads": 2 * B + 2 + 2 * B + 6 + 2 * B, "weigh": B, "sum": B}[mode]
                    if mode == "heads":
                        PER = B + 1 + 2 + 2 + 1 + 2 * B + 3 + 2 * B
                    if mode == "attend":
                        PER = B + 1 + 1 + 1 + 2 * B + 3 + B
                    with dve.Fori(0, pairs) as i:
                        for q in range(2):
                            own = Steps(dve, m["own"], i * (2 * PER) + q * PER)
                            dve.wait_ge(listed[q], i * 32 + 32)
                            dve.sem_inc(m["dve_passed"], 1)
                            tk = [dve.value_load(tiles[q][0:1, b:b + 1], min_val=0, max_val=T - 1) for b in range(B)]
                            if soft:
                                for b in range(B):
                                    js = slice(b * J, b * J + J)
                                    dve.wait_ge(got[q][b], i * (16 * J) + 16 * J)
                                    if mode == "attend":
                                        own(dve.tensor_tensor(prod[:, js, :], rows[q][:, js, :],
                                                              k.q[:, ds(tk[b], 1), :].to_broadcast([P, J, P + 1]), ALU.mult))
                                    else:
                                        own(dve.tensor_tensor(prod[:, js, :], rows[q][:, js, 0:P],
                                                              k.q[:, ds(tk[b], 1), 0:P].to_broadcast([P, J, P]), ALU.mult))
                                own.wait()
                                if mode == "attend":
                                    own(dve.tensor_reduce(score[:, :, 0], prod[:], AX.X, ALU.add))
                                    own.wait()
                                    own(dve.tensor_tensor(expo[:, 0:S, 0], score[:, :, 0], meta[q][:, :, 2], ALU.add))
                                    own.wait()
                                else:
                                    own(dve.tensor_reduce(score[:, :, 0:8],
                                                          prod[:].rearrange("p s (h d) -> p s h d", d=D_HEAD), AX.X, ALU.add))
                                    own(dve.tensor_scalar(masks[:, :, 0], meta[q][:, :, 3], 1.0, -BIG, ALU.not_equal, ALU.mult))
                                    own(dve.tensor_scalar(masks[:, :, 1], meta[q][:, :, 3], 0.0, -BIG, ALU.not_equal, ALU.mult))
                                    own.wait()
                                    for r in range(2):
                                        own(dve.tensor_tensor(expo[:, 0:S, r * 8:r * 8 + 8], score[:, :, 0:8],
                                                              masks[:, :, r:r + 1].to_broadcast([P, S, 8]), ALU.add))
                                    own.wait()
                                own(dve.tensor_reduce(nmb[:], expo[:, 0:S, :].rearrange("p (b j) r -> p b r j", j=J),
                                                      AX.X, ALU.max, negate=True))
                                own.wait()
                                for b in range(B):
                                    own(dve.tensor_copy(nmo[:, b, :], k.nm[:, ds(tk[b], 1), 0:R].rearrange("p a r -> p (a r)")))
                                    own.wait()
                                    own(dve.tensor_tensor(k.nm[:, ds(tk[b], 1), 0:R].rearrange("p a r -> p (a r)"),
                                                          nmo[:, b, :], nmb[:, b, :], ALU.min))
                                    own.wait()
                                own(dve.tensor_tensor(nmn[:], nmo[:], nmb[:], ALU.min))
                                own.wait()
                                own(dve.tensor_tensor(expo[:, 0:S, :].rearrange("p (b j) r -> p b j r", j=J),
                                                      expo[:, 0:S, :].rearrange("p (b j) r -> p b j r", j=J),
                                                      nmn[:].unsqueeze(2).to_broadcast([P, B, J, R]), ALU.add))
                                own(dve.tensor_tensor(expo[:, S:S + B, :], nmn[:], nmo[:], ALU.subtract))
                                own.wait()
                                dve.sem_inc(m["scored"], 1)
                                dve.sem_inc(read[q], 1)
                            if mode == "heads":
                                dve.wait_ge(m["powered"], i * 4 + (q * 2 + 2))
                                wv = wide[:].rearrange("p s (r d) -> p s r d", d=D_HEAD + 1)
                                for r in range(2):
                                    ins = dve.tensor_tensor(
                                        wv[:, :, r * 8:r * 8 + 8, 0:D_HEAD],
                                        rows[q][:, :, P:2 * P].rearrange("p s (h d) -> p s h d", d=D_HEAD),
                                        wv[:, :, r * 8:r * 8 + 8, D_HEAD:D_HEAD + 1].to_broadcast([P, S, 8, D_HEAD]), ALU.mult)
                                ins.then_inc(m["weighted"], 1)
                            dve.wait_ge(m["summed"], i * 2 + (q + 2))
                            dve.sem_inc(released[q], 1)
                            if not soft:
                                dve.sem_inc(read[q], 1)
                            for b in range(B):
                                a = k.acc[:, ds(tk[b], 1), 0:W].rearrange("p a w -> p (a w)")
                                if mode == "attend":
                                    own(dve.scalar_tensor_tensor(a, a, corr[:, S + b, :], total[:, b, 0:W], ALU.mult, ALU.add))
                                elif mode == "heads":
                                    kh = kept[:].rearrange("p (r d) -> p r d", d=D_HEAD + 1)
                                    own(dve.tensor_tensor(kh, a.rearrange("p (r d) -> p r d", d=D_HEAD + 1),
                                                          corr[:, S + b, :].unsqueeze(2).to_broadcast([P, R, D_HEAD + 1]), ALU.mult))
                                    own.wait()
                                    own(dve.tensor_tensor(a, kept[:], total[:, b, 0:W], ALU.add))
                                else:
                                    own(dve.tensor_tensor(a, a, total[:, b, 0:W], ALU.add))
                                own.wait()
                            dve.sem_inc(m["sum_taken"], 1)
                            assert own.n == PER, (own.n, PER)
            close_stage(nc, m)


GT = 7
NGT = T // GT
EPS = 1e-5


def scatter_rows(pool, k, m, rows, table_d, bound=NPAD - 1, skip=True):
    for t in range(T):
        pool.indirect_dma_start(table_d, bass.IndirectOffsetOnAxis(k.perm[:, t:t + 1], 0), rows[:, t, :], None,
                                bounds_check=bound, oob_is_err=False).then_inc(m["scattered"], 16)
    pool.wait_ge(m["scattered"], 16 * T)


def norm_steps(dve, own, m, b, x):
    for j in range(GT):
        own(dve.bn_stats(b.stats[:, j, :], x(j)))
    own.wait()
    dve.sem_inc(m["passed"], 1)
    for j in range(GT):
        own(dve.bn_aggr(b.mv[:, j, :], b.stats[:, j, :]))
    own.wait()


def linear(nc, k, prepare, weights, finish, width=P, names=(), per_prepare=0, per_finish=0, extra=None, bias=None,
           act_extra=None, late_root=False):
    n = len(weights)
    stride = P if width <= P else 256
    with ExitStack() as s:
        m = open_stage(nc, s, ["own", "prepared", "turned_ps", "turned", "multiplied", "act_own", "to_act", "from_act",
                               "scattered", *names])
        b = Bag()
        b.a = [buf(nc, s, f"lin_a{r}", [P, GT, P]) for r in range(n)]
        b.at = [buf(nc, s, f"lin_at{r}", [P, GT, P]) for r in range(n)]
        b.t1 = buf(nc, s, "lin_t1", [P, GT, P])
        b.stats = buf(nc, s, "lin_stats", [P, GT, 6])
        b.mv = buf(nc, s, "lin_mv", [P, GT, 2])
        b.rstd = buf(nc, s, "lin_rstd", [P, GT])
        b.nb = buf(nc, s, "lin_nb", [P, GT])
        b.small = buf(nc, s, "lin_small", [P, GT, 16])
        turned_ps = psum(nc, s, "lin_turned", [P, 8, P], F32)
        b.out = psum(nc, s, "lin_out", [P, 8, stride], F32)
        with nc.Block() as block:
            @block.vector
            def _(dve):
                own = Steps(dve, m["own"])
                with dve.Fori(0, NGT) as g:
                    own.first, own.n = g * (per_prepare + per_finish), 0
                    prepare(dve, own, m, b, g)
                    assert own.n == per_prepare, own.n
                    own.wait()
                    dve.sem_inc(m["prepared"], 1)
                    dve.wait_ge(m["multiplied"], g + 1)
                    finish(dve, own, m, b, g)
                    assert own.n == per_prepare + per_finish, own.n
                    own.wait()
                    for name in names:
                        dve.sem_inc(m[name], 1)

            @block.tensor
            def _(pe):
                with pe.Fori(0, NGT) as g:
                    pe.wait_ge(m["prepared"], g + 1)
                    for r in range(n):
                        if r:
                            pe.wait_ge(m["turned"], g * n + r)
                        for j in range(GT):
                            mm = pe.transpose(turned_ps[:, j, :], b.a[r][:, j, :], k.ident[:])
                        mm.then_inc(m["turned_ps"], 1)
                    pe.wait_ge(m["turned"], g * n + n)
                    for j in range(GT):
                        for r in range(n):
                            mm = pe.matmul(b.out[:, j, 0:width], b.at[r][:, j, :], weights[r], start=(r == 0),
                                           stop=(r == n - 1 and bias is None))
                        if bias is not None:
                            mm = pe.matmul(b.out[:, j, 0:width], k.ones[0:1, :], bias, start=False, stop=True)
                    mm.then_inc(m["multiplied"], 1)

            @block.scalar
            def _(act):
                with act.Fori(0, NGT) as g:
                    if act_extra is not None:
                        act_extra(act, m, b, g)
                    for r in range(n):
                        act.wait_ge(m["turned_ps"], g * n + (r + 1))
                        act.copy(b.at[r][:], turned_ps[:, 0:GT, :]).then_inc(m["turned"], 1)
                    if late_root:
                        act.wait_ge(m["to_act"], g + 1)
                        act.activation(b.rstd[:], b.mv[:, :, 1], ACT.Sqrt, bias=k.eps[:]).then_inc(m["from_act"], 1)

            if extra is not None:
                @block.gpsimd
                def _(pool):
                    extra(pool, m)
        close_stage(nc, m)


def tl(array, g, w=None):
    return array[:, ds(g * GT, GT), :] if w is None else array[:, ds(g * GT, GT), 0:w]


def norm_act(k, relu_to):
    def part(act, m, b, g):
        act.wait_ge(m["to_act"], g * 2 + 1)
        act.activation(b.rstd[:], b.mv[:, :, 1], ACT.Sqrt, bias=k.eps[:]).then_inc(m["from_act"], 1)
        act.wait_ge(m["to_act"], g * 2 + 2)
        for j in range(GT):
            ins = act.activation(relu_to(b)[:, j, :], b.t1[:, j, :], ACT.Relu, bias=b.nb[:, j:j + 1], scale=b.rstd[:, j:j + 1])
        ins.then_inc(m["from_act"], 1)
    return part


NORM = 1 + 2 * GT + 2


def norm_dve(dve, own, m, b, g, x):
    own(dve.tensor_copy(b.t1[:], x))
    own.wait()
    norm_steps(dve, own, m, b, lambda j: b.t1[:, j, :])
    dve.sem_inc(m["to_act"], 1)
    dve.wait_ge(m["from_act"], g * 2 + 1)
    own(dve.reciprocal(b.rstd[:], b.rstd[:]))
    own.wait()
    own(dve.scalar_tensor_tensor(b.nb[:], b.mv[:, :, 0], -1.0, b.rstd[:], ALU.mult, ALU.mult))
    own.wait()
    dve.sem_inc(m["to_act"], 1)
    dve.wait_ge(m["from_act"], g * 2 + 2)


def load_weights(nc, k, pairs):
    with ExitStack() as s:
        m = open_stage(nc, s, ["loaded"])
        with nc.Block() as block:
            @block.sync
            def _(sp):
                for out, src in pairs:
                    sp.dma_start(out, src).then_inc(m["loaded"], 16)
                sp.wait_ge(m["loaded"], 16 * len(pairs))
        close_stage(nc, m)


def row(v, l=None):
    return v.rearrange("(a n) -> a n", a=1)


def layer_weights(nc, k, I, l):
    with ExitStack() as s:
        m = open_stage(nc, s, ["loaded", "turned_ps", "turned", "made_ps", "own", "made"])
        w = {n: buf(nc, s, f"w_{n}", [P, P]) for n in ("WQ", "WK", "WV", "WO")}
        wt = {n: buf(nc, s, f"wt_{n}", [P, P + 1]) for n in ("WQ", "WK", "WV")}
        bq = buf(nc, s, "bq_col", [P, 1])
        bv = buf(nc, s, "bv_col", [P, 1])
        bvb = buf(nc, s, "bv_cols", [P, P])
        ps = psum(nc, s, "lw_turned", [P, 4, P], F32)
        out = psum(nc, s, "lw_out", [P, 4, 512], F32)
        with nc.Block() as block:
            @block.sync
            def _(sp):
                for n in w:
                    sp.dma_start(w[n][:], I[f"L0_gnn_{n}"][ds(l, 1)].rearrange("a i j -> (a i) j")).then_inc(m["loaded"], 16)
                for n, o in (("bQ", bq[:]), ("bV", bv[:]), ("bK", wt["WK"][:, P:P + 1])):
                    sp.dma_start(o, I[f"L0_gnn_{n}"][ds(l, 1)].rearrange("a (p n) -> (a p) n", n=1),
                                 allow_slow_non_contiguous=True).then_inc(m["loaded"], 16)
                sp.dma_start(k.bo[:], I["L0_gnn_bO"][ds(l, 1)]).then_inc(m["loaded"], 16)
                for n, o in (("ln_g", k.gb), ("ln_b", k.bb)):
                    sp.dma_start(o[:], I[f"L0_gnn_{n}"][ds(l, 1)].rearrange("a n -> (a n)").partition_broadcast(P)).then_inc(m["loaded"], 16)
                sp.wait_ge(m["loaded"], 160)

            @block.tensor
            def _(pe):
                pe.wait_ge(m["loaded"], 160)
                for r, n in enumerate(("WQ", "WK", "WV")):
                    mm = pe.transpose(ps[:, r, :], w[n][:], k.ident[:])
                mm.then_inc(m["turned_ps"], 1)
                pe.wait_ge(m["turned"], 4)
                pe.matmul(out[:, 0, 0:P + 1], wt["WQ"][:, 0:P], wt["WK"][:], start=True, stop=True)
                pe.matmul(out[0:1, 1, 0:P + 1], bq[:], wt["WK"][:], start=True, stop=True)
                pe.matmul(out[:, 2, 0:P], wt["WV"][:, 0:P], w["WO"][:], start=True, stop=True)
                pe.matmul(out[:, 3, 0:P], bvb[:], w["WO"][:], start=True, stop=True).then_inc(m["made_ps"], 1)

            @block.vector
            def _(dve):
                dve.wait_ge(m["loaded"], 160)
                dve.tensor_copy(bvb[:], bv[:].to_broadcast([P, P])).then_inc(m["turned"], 1)
                dve.wait_ge(m["turned_ps"], 1)
                for r, n in enumerate(("WQ", "WK", "WV")):
                    dve.tensor_copy(wt[n][:, 0:P], ps[:, r, :]).then_inc(m["turned"], 1)
                dve.wait_ge(m["made_ps"], 1)
                scale = 1.0 / float(np.sqrt(P))
                dve.tensor_scalar(k.wz[:], out[:, 0, 0:P + 1], scale, None, ALU.mult)
                dve.tensor_scalar(k.bz[:], out[0:1, 1, 0:P + 1], scale, None, ALU.mult)
                dve.tensor_copy(k.wvo[:], out[:, 2, 0:P])
                dve.tensor_copy(k.bvo[:], out[:, 3, 0:P])
        close_stage(nc, m)


def embed(nc, k):
    def prepare(dve, own, m, b, g):
        norm_dve(dve, own, m, b, g, tl(k.x, g))

    def finish(dve, own, m, b, g):
        own(dve.tensor_copy(tl(k.h, g), b.out[:, 0:GT, :]))
    linear(nc, k, prepare, [k.w1[:]], finish, bias=k.b1[:], per_prepare=NORM, per_finish=1,
           act_extra=norm_act(k, lambda b: b.a[0]))


def project(nc, k):
    def prepare(dve, own, m, b, g):
        own(dve.tensor_copy(b.a[0][:], tl(k.h, g)))

    def finish(dve, own, m, b, g):
        own(dve.tensor_copy(tl(k.q, g), b.out[:, 0:GT, 0:P + 1]))
    linear(nc, k, prepare, [k.wz[:]], finish, width=P + 1, bias=k.bz[:], per_prepare=1, per_finish=1,
           extra=lambda pool, m: scatter_rows(pool, k, m, k.h, k.table_d))


def update(nc, k):
    def prepare(dve, own, m, b, g):
        own(dve.tensor_scalar(b.small[:, :, 0], k.acc[:, ds(g * GT, GT), P:P + 1].rearrange("p t a -> p (t a)"), 0.5, None, ALU.max))
        own.wait()
        own(dve.reciprocal(b.small[:, :, 1], b.small[:, :, 0]))
        own.wait()
        own(dve.tensor_tensor(b.a[0][:], tl(k.acc, g, P), b.small[:, :, 1:2].to_broadcast([P, GT, P]), ALU.mult))
        own(dve.tensor_tensor(b.small[:, :, 2:3], k.acc[:, ds(g * GT, GT), P:P + 1], b.small[:, :, 1:2], ALU.mult))

    def finish(dve, own, m, b, g):
        own(dve.tensor_tensor(b.t1[:], b.out[:, 0:GT, :], tl(k.h, g), ALU.add))
        own.wait()
        for j in range(GT):
            own(dve.scalar_tensor_tensor(b.t1[:, j, :], k.bvo[:], b.small[:, j, 2:3], b.t1[:, j, :], ALU.mult, ALU.add))
        own.wait()
        norm_steps(dve, own, m, b, lambda j: b.t1[:, j, :])
        dve.sem_inc(m["to_act"], 1)
        dve.wait_ge(m["from_act"], g + 1)
        own(dve.reciprocal(b.rstd[:], b.rstd[:]))
        own.wait()
        for j in range(GT):
            own(dve.tensor_scalar(b.t1[:, j, :], b.t1[:, j, :], b.mv[:, j, 0:1], b.rstd[:, j:j + 1], ALU.subtract, ALU.mult))
        own.wait()
        own(dve.tensor_tensor(b.t1[:], b.t1[:], k.gb[:].unsqueeze(1).to_broadcast([P, GT, P]), ALU.mult))
        own.wait()
        own(dve.tensor_tensor(tl(k.h, g), b.t1[:], k.bb[:].unsqueeze(1).to_broadcast([P, GT, P]), ALU.add))

    linear(nc, k, prepare, [k.wvo[:]], finish, bias=k.bo[:], per_prepare=4, per_finish=1 + GT + 2 * GT + 1 + GT + 2,
           late_root=True)


def copy_out(nc, k):
    def prepare(dve, own, m, b, g):
        own(dve.tensor_copy(b.a[0][:], tl(k.h, g)))

    def finish(dve, own, m, b, g):
        own(dve.tensor_tensor(tl(k.x, g), b.out[:, 0:GT, :], tl(k.x, g), ALU.add))
    linear(nc, k, prepare, [k.w1[:]], finish, bias=k.b1[:], per_prepare=1, per_finish=1)


def norm_only(nc, k, out, extra=None, scale=None):
    with ExitStack() as s:
        m = open_stage(nc, s, ["own", "to_act", "from_act", "scattered", "done"])
        b = Bag()
        b.a = [buf(nc, s, "no_a", [P, GT, P])]
        b.t1 = buf(nc, s, "no_t1", [P, GT, P])
        b.stats = buf(nc, s, "no_stats", [P, GT, 6])
        b.mv = buf(nc, s, "no_mv", [P, GT, 2])
        b.rstd = buf(nc, s, "no_rstd", [P, GT])
        b.nb = buf(nc, s, "no_nb", [P, GT])
        with nc.Block() as block:
            @block.vector
            def _(dve):
                own = Steps(dve, m["own"])
                with dve.Fori(0, NGT) as g:
                    own.first, own.n = g * (NORM + 1), 0
                    norm_dve(dve, own, m, b, g, tl(k.x, g))
                    if scale is None:
                        own(dve.tensor_copy(tl(out, g), b.a[0][:]))
                    else:
                        own(dve.tensor_tensor(tl(out, g), b.a[0][:], scale[:, ds(g * GT, GT)].unsqueeze(2).to_broadcast([P, GT, P]), ALU.mult))
                    own.wait()
                    dve.sem_inc(m["done"], 1)

            @block.scalar
            def _(act):
                part = norm_act(k, lambda b: b.a[0])
                with act.Fori(0, NGT) as g:
                    part(act, m, b, g)

            @block.gpsimd
            def _(pool):
                for t in range(T):
                    if t % GT == 0:
                        pool.wait_ge(m["done"], t // GT + 1)
                    pool.indirect_dma_start(k.table_d, bass.IndirectOffsetOnAxis(k.perm[:, t:t + 1], 0), out[:, t, :], None,
                                            bounds_check=NPAD - 1, oob_is_err=False).then_inc(m["scattered"], 16)
                pool.wait_ge(m["scattered"], 16 * T)
        close_stage(nc, m)


def heads_weights(nc, k, I):
    with ExitStack() as s:
        m = open_stage(nc, s, ["blank", "loaded", "scaled", "turned_ps", "turned", "made_ps"])
        wk = buf(nc, s, "hw_k", [P, P])
        wv = buf(nc, s, "hw_v", [P, P])
        wkt = buf(nc, s, "hw_kt", [P, P])
        wvt = buf(nc, s, "hw_vt", [P, P])
        bk = buf(nc, s, "hw_bk", [P, 1])
        bv = buf(nc, s, "hw_bv", [P, 1])
        mix = buf(nc, s, "hw_mix", [P, 4, P])
        pr = buf(nc, s, "hw_p", [P, 2, 8])
        pr4 = buf(nc, s, "hw_p4", [P, 2, 8])
        ps = psum(nc, s, "hw_turned", [P, 4, P], F32)
        out = psum(nc, s, "hw_out", [P, 512], F32)
        outb = psum(nc, s, "hw_outb", [1, 512], F32)
        with nc.Block() as block:
            @block.gpsimd
            def _(pool):
                pool.memset(mix[:], 0.0).then_inc(m["blank"], 1)

            @block.sync
            def _(sp):
                sp.wait_ge(m["blank"], 1)
                for r in range(2):
                    for h in range(8):
                        d = slice(h * D_HEAD, (h + 1) * D_HEAD)
                        sp.dma_start(mix[d, 2 * r, d], I["L1_gnn_a_rel"][r, h]).then_inc(m["loaded"], 16)
                        sp.dma_start(mix[d, 2 * r + 1, d], I["L1_gnn_m_rel"][r, h]).then_inc(m["loaded"], 16)
                sp.dma_start(pr[:].rearrange("p r h -> p (r h)"),
                             I["L1_gnn_p_rel"].rearrange("r h -> (r h)").partition_broadcast(P)).then_inc(m["loaded"], 16)
                for o, n in ((wk[:], "Wk"), (wv[:], "Wv"), (k.w1[:], "Wq")):
                    sp.dma_start(o, I[f"L1_gnn_{n}"]).then_inc(m["loaded"], 16)
                for o, n in ((bk[:], "bk"), (bv[:], "bv")):
                    sp.dma_start(o, I[f"L1_gnn_{n}"].rearrange("(p n) -> p n", n=1), allow_slow_non_contiguous=True
                                 ).then_inc(m["loaded"], 16)
                sp.dma_start(k.b1[:], row(I["L1_gnn_bq"])).then_inc(m["loaded"], 16)
                sp.wait_ge(m["loaded"], 16 * 39)

            @block.vector
            def _(dve):
                dve.wait_ge(m["loaded"], 16 * 39)
                dve.tensor_scalar(pr4[:], pr[:], float(D_HEAD) ** -0.5, None, ALU.mult).then_inc(m["scaled"], 1)
                dve.wait_ge(m["scaled"], 1)
                for r in range(2):
                    a = mix[:, 2 * r, :].rearrange("p (h d) -> p h d", d=D_HEAD)
                    dve.tensor_tensor(a, a, pr4[:, r, :].unsqueeze(2).to_broadcast([P, 8, D_HEAD]), ALU.mult).then_inc(m["scaled"], 1)
                dve.wait_ge(m["turned_ps"], 1)
                dve.tensor_copy(wkt[:], ps[:, 0, :]).then_inc(m["turned"], 1)
                dve.tensor_copy(wvt[:], ps[:, 1, :]).then_inc(m["turned"], 1)
                dve.wait_ge(m["made_ps"], 1)
                dve.tensor_copy(k.wkv[:], out[:])
                dve.tensor_copy(k.bkv[:], outb[:])

            @block.tensor
            def _(pe):
                pe.wait_ge(m["loaded"], 16 * 39)
                pe.transpose(ps[:, 0, :], wk[:], k.ident[:])
                pe.transpose(ps[:, 1, :], wv[:], k.ident[:]).then_inc(m["turned_ps"], 1)
                pe.wait_ge(m["turned"], 2)
                pe.wait_ge(m["scaled"], 3)
                for c in range(4):
                    wt, bc = ((wkt, bk), (wvt, bv))[c % 2]
                    pe.matmul(out[:, c * P:(c + 1) * P], wt[:], mix[:, c, :], start=True, stop=True)
                    mm = pe.matmul(outb[:, c * P:(c + 1) * P], bc[:], mix[:, c, :], start=True, stop=True)
                mm.then_inc(m["made_ps"], 1)
        close_stage(nc, m)


def heads_project(nc, k):
    with ExitStack() as s:
        m = open_stage(nc, s, ["own", "to_act", "from_act", "prepared", "turned_ps", "turned", "multiplied", "kv_ps", "kv_sb",
                               "kv_taken", "kv_free", "scattered"])
        b = Bag()
        b.a = [buf(nc, s, "hp_a", [P, GT, P])]
        at = buf(nc, s, "hp_at", [P, GT, P])
        b.t1 = buf(nc, s, "hp_t1", [P, GT, P])
        b.stats = buf(nc, s, "hp_stats", [P, GT, 6])
        b.mv = buf(nc, s, "hp_mv", [P, GT, 2])
        b.rstd = buf(nc, s, "hp_rstd", [P, GT])
        b.nb = buf(nc, s, "hp_nb", [P, GT])
        kv = buf(nc, s, "hp_kv", [P, GT, 4 * P])
        turned_ps = psum(nc, s, "hp_turned", [P, 8, P], F32)
        q_ps = psum(nc, s, "hp_q", [P, 8, P], F32)
        kv_ps = psum(nc, s, "hp_kvps", [P, 2, 4 * P], F32)
        with nc.Block() as block:
            @block.vector
            def _(dve):
                own = Steps(dve, m["own"])
                with dve.Fori(0, NGT) as g:
                    own.first, own.n = g * (NORM + 2), 0
                    norm_dve(dve, own, m, b, g, tl(k.x, g))
                    dve.sem_inc(m["prepared"], 1)
                    own(dve.tensor_copy(tl(k.h, g), b.a[0][:]))
                    dve.wait_ge(m["multiplied"], g + 1)
                    own(dve.tensor_copy(tl(k.q, g, P), q_ps[:, 0:GT, :]))
                    own.wait()

            @block.tensor
            def _(pe):
                pe.nop().then_inc(m["kv_taken"], 2)
                with pe.Fori(0, NGT) as g:
                    pe.wait_ge(m["prepared"], g + 1)
                    for j in range(GT):
                        mm = pe.transpose(turned_ps[:, j, :], b.a[0][:, j, :], k.ident[:])
                    mm.then_inc(m["turned_ps"], 1)
                    pe.wait_ge(m["turned"], g + 1)
                    for j in range(GT):
                        pe.matmul(q_ps[:, j, :], at[:, j, :], k.w1[:], start=True, stop=False)
                        mm = pe.matmul(q_ps[:, j, :], k.ones[0:1, :], k.b1[:], start=False, stop=True)
                    mm.then_inc(m["multiplied"], 1)
                    for j in range(GT):
                        pe.wait_ge(m["kv_taken"], g * GT + (j + 1))
                        pe.matmul(kv_ps[:, j % 2, :], at[:, j, :], k.wkv[:], start=True, stop=False)
                        pe.matmul(kv_ps[:, j % 2, :], k.ones[0:1, :], k.bkv[:], start=False, stop=True).then_inc(m["kv_ps"], 1)

            @block.scalar
            def _(act):
                part = norm_act(k, lambda b: b.a[0])
                act.nop().then_inc(m["kv_free"], 1)
                with act.Fori(0, NGT) as g:
                    part(act, m, b, g)
                    act.wait_ge(m["turned_ps"], g + 1)
                    act.copy(at[:], turned_ps[:, 0:GT, :]).then_inc(m["turned"], 1)
                    act.wait_ge(m["kv_free"], g + 1)
                    for j in range(GT):
                        act.wait_ge(m["kv_ps"], g * GT + (j + 1))
                        act.copy(kv[:, j, :], kv_ps[:, j % 2, :]).then_inc(m["kv_taken"], 1)

            @block.gpsimd
            def _(pool):
                for t in range(T):
                    pool.wait_ge(m["kv_taken"], t + 3)
                    for r in range(2):
                        pool.indirect_dma_start(k.pairs_d, bass.IndirectOffsetOnAxis((k.perm, k.perm1)[r][:, t:t + 1], 0),
                                                kv[:, t % GT, r * 2 * P:(r + 1) * 2 * P], None, bounds_check=2 * NPAD - 1,
                                                oob_is_err=False).then_inc(m["scattered"], 16)
                    if t % GT == GT - 1:
                        pool.wait_ge(m["scattered"], 32 * (t + 1))
                        pool.sem_inc(m["kv_free"], 1)
        close_stage(nc, m)


def heads_out(nc, k):
    def prepare(dve, own, m, b, g):
        acc = k.acc[:, ds(g * GT, GT), :].rearrange("p t (r d) -> p t r d", d=D_HEAD + 1)
        own(dve.tensor_scalar(b.small[:], acc[:, :, :, D_HEAD], 0.5, None, ALU.max))
        own.wait()
        own(dve.reciprocal(b.small[:], b.small[:]))
        own.wait()
        for r in range(2):
            for j in range(GT):
                own(dve.tensor_tensor(k.two[:, r, j, :].rearrange("p (h d) -> p h d", d=D_HEAD),
                                      k.acc[:, ds(g * GT + j, 1), :].rearrange("p t (r d) -> p (t r) d", d=D_HEAD + 1)
                                      [:, r * 8:r * 8 + 8, 0:D_HEAD],
                                      b.small[:, j, r * 8:r * 8 + 8].unsqueeze(2).to_broadcast([P, 8, D_HEAD]), ALU.mult))
        own.wait()
        own(dve.tensor_tensor(b.t1[:], k.two[:, 0], k.two[:, 1], ALU.add))
        own.wait()
        dve.sem_inc(m["to_act"], 1)
        dve.wait_ge(m["from_act"], g + 1)

    def gelu(act, m, b, g):
        act.wait_ge(m["to_act"], g + 1)
        act.activation(b.a[0][:], b.t1[:], ACT.Gelu).then_inc(m["from_act"], 1)

    def finish(dve, own, m, b, g):
        own(dve.scalar_tensor_tensor(b.t1[:], tl(k.h, g), k.gate[:, 1:2], tl(k.x, g), ALU.mult, ALU.add))
        own.wait()
        own(dve.scalar_tensor_tensor(tl(k.x, g), b.out[:, 0:GT, :], k.gate[:, 0:1], b.t1[:], ALU.mult, ALU.add))
    linear(nc, k, prepare, [k.w1[:]], finish, bias=k.b1[:], per_prepare=2 + 2 * GT + 1, per_finish=2, act_extra=gelu)


def gate_columns(nc, k, skip):
    with ExitStack() as s:
        m = open_stage(nc, s, ["loaded", "own", "powered"])
        t = buf(nc, s, "gate_t", [P, 3])
        with nc.Block() as block:
            @block.sync
            def _(sp):
                sp.dma_start(t[:, 0:1], skip.partition_broadcast(P)).then_inc(m["loaded"], 16)

            @block.scalar
            def _(act):
                act.wait_ge(m["loaded"], 16)
                act.activation(t[:, 1:2], t[:, 0:1], ACT.Exp, scale=-1.0).then_inc(m["powered"], 1)

            @block.vector
            def _(dve):
                own = Steps(dve, m["own"])
                dve.wait_ge(m["powered"], 1)
                own(dve.tensor_scalar(t[:, 2:3], t[:, 1:2], 1.0, None, ALU.add))
                own.wait()
                own(dve.reciprocal(k.gate[:, 0:1], t[:, 2:3]))
                own.wait()
                own(dve.tensor_scalar(k.gate[:, 1:2], k.gate[:, 0:1], -1.0, 1.0, ALU.mult, ALU.add))
                own.wait()
        close_stage(nc, m)


def resort(nc, k, rows_d, perm_to):
    with ExitStack() as s:
        m = open_stage(nc, s, ["scattered", "gathered"])
        with nc.Block() as block:
            @block.gpsimd
            def _(pool):
                for t in range(T):
                    pool.indirect_dma_start(rows_d, bass.IndirectOffsetOnAxis(k.perm[:, t:t + 1], 0), k.x[:, t, :], None,
                                            bounds_check=NPAD - 1, oob_is_err=False).then_inc(m["scattered"], 16)
                pool.wait_ge(m["scattered"], 16 * T)
                gather_rows(pool, m, k.x, rows_d, perm_to, NPAD - 1)
        close_stage(nc, m)


def gather_rows(pool, m, out, rows_d, perm, bound):
    for t in range(T):
        pool.indirect_dma_start(out[:, t, :], None, rows_d, bass.IndirectOffsetOnAxis(perm[:, t:t + 1], 0),
                                bounds_check=bound, oob_is_err=False).then_inc(m["gathered"], 16)
    pool.wait_ge(m["gathered"], 16 * T)


def load_nodes(nc, k, x_d):
    with ExitStack() as s:
        m = open_stage(nc, s, ["blank", "gathered"])
        with nc.Block() as block:
            @block.vector
            def _(dve):
                dve.memset(k.x[:], 0.0).then_inc(m["blank"], 1)
                dve.tensor_scalar(k.perm1[:], k.perm[:], float(NPAD), None, ALU.add)

            @block.gpsimd
            def _(pool):
                pool.wait_ge(m["blank"], 1)
                gather_rows(pool, m, k.x, x_d, k.perm, N - 1)
        close_stage(nc, m)


def mean_out(nc, k):
    def prepare(dve, own, m, b, g):
        own(dve.tensor_copy(b.a[0][:], tl(k.h, g)))
        own(dve.tensor_tensor(b.a[1][:], tl(k.acc, g, P), k.inv[:, ds(g * GT, GT)].unsqueeze(2).to_broadcast([P, GT, P]), ALU.mult))

    def finish(dve, own, m, b, g):
        own(dve.tensor_tensor(tl(k.x, g), b.out[:, 0:GT, :], tl(k.x, g), ALU.add))
    linear(nc, k, prepare, [k.w1[:], k.w2[:]], finish, bias=k.b1[:], per_prepare=2, per_finish=1)


def degree_columns(nc, k):
    with ExitStack() as s:
        m = open_stage(nc, s, ["own", "rooted"])
        t = buf(nc, s, "deg_t", [P, 3, T])
        with nc.Block() as block:
            @block.vector
            def _(dve):
                own = Steps(dve, m["own"])
                own(dve.tensor_scalar(t[:, 0, :], k.deg_s[:], 1.0, None, ALU.max))
                own.wait()
                own(dve.reciprocal(k.inv[:], t[:, 0, :]))
                dve.wait_ge(m["rooted"], 1)
                own(dve.reciprocal(t[:, 2, :], t[:, 1, :]))
                own.wait()
                own(dve.scalar_tensor_tensor(k.dis[:], k.deg_s[:], 0.0, t[:, 2, :], ALU.is_gt, ALU.mult))
                own.wait()

            @block.scalar
            def _(act):
                act.wait_ge(m["own"], 1)
                act.activation(t[:, 1, :], t[:, 0, :], ACT.Sqrt).then_inc(m["rooted"], 1)
        close_stage(nc, m)


def turn_weight(nc, k, w_d):
    with ExitStack() as s:
        m = open_stage(nc, s, ["loaded", "turned"])
        w = buf(nc, s, "tw_w", [P, P])
        ps = psum(nc, s, "tw_ps", [P, P], F32)
        with nc.Block() as block:
            @block.sync
            def _(sp):
                sp.dma_start(w[:], w_d).then_inc(m["loaded"], 16)

            @block.tensor
            def _(pe):
                pe.wait_ge(m["loaded"], 16)
                pe.transpose(ps[:], w[:], k.ident[:]).then_inc(m["turned"], 1)

            @block.vector
            def _(dve):
                dve.wait_ge(m["turned"], 1)
                dve.tensor_copy(k.w1[:], ps[:])
        close_stage(nc, m)


def final_out(nc, k, out_d):
    def prepare(dve, own, m, b, g):
        own(dve.tensor_tensor(b.a[0][:], tl(k.acc, g, P), k.dis[:, ds(g * GT, GT)].unsqueeze(2).to_broadcast([P, GT, P]), ALU.mult))

    def finish(dve, own, m, b, g):
        own(dve.tensor_tensor(tl(k.x, g), b.out[:, 0:GT, :], tl(k.x, g), ALU.add))

    def store(pool, m):
        for t in range(T):
            if t % GT == 0:
                pool.wait_ge(m["stored"], t // GT + 1)
            pool.indirect_dma_start(out_d, bass.IndirectOffsetOnAxis(k.perm[:, t:t + 1], 0), k.x[:, t, :], None,
                                    bounds_check=N - 1, oob_is_err=False).then_inc(m["scattered"], 16)
        pool.wait_ge(m["scattered"], 16 * T)
    linear(nc, k, prepare, [k.w1[:]], finish, bias=k.b1[:], per_prepare=1, per_finish=1, names=("stored",), extra=store)


def gnn_kernel(nc, I, out_d):
    with ExitStack() as c:
        k = Bag()
        dram = lambda n, shape, dt=F32: nc.dram_tensor(n, shape, dt, kind="Internal").ap()
        k.layers = I["L0_gnn_WQ"].shape[0]
        k.scrap_d = dram("scrap_d", [2, P, REC])
        k.table_d = dram("table_d", [NPAD, P])
        k.pairs_d = dram("pairs_d", [2 * NPAD, 2 * P])
        rows_d = dram("rows_d", [NPAD, P])
        constants(nc, c, k)
        lists = {}
        for w in ("in", "out"):
            L = Bag()
            L.perm = buf(nc, c, f"perm_{w}", [P, T], I32)
            L.deg = buf(nc, c, f"deg_{w}", [P, T])
            L.sched = buf(nc, c, f"sched_{w}", [1, SCHED], I32)
            L.list_d = dram(f"list_{w}_d", [NG * P * S, REC])
            L.tiles_d = dram(f"tiles_{w}_d", [P * NBLK], I32)
            L.perm_d = dram(f"perm_{w}_d", [NPAD, 2])
            L.keys_d = dram(f"keys_{w}_d", [NPAD])
            lists[w] = L
        with ExitStack() as p:
            edge_layout(nc, p, k, I["src"], I["dst"], I["edge_type_2"], I["edge_weight1"].rearrange("e a -> (e a)"))
            k.lo = buf(nc, p, "lo", [P, ECOL], BF16)
            k.hi = buf(nc, p, "hi", [P, ECOL], BF16)
            oh = [buf(nc, p, f"oh{q}", [P, CH, P + T], BF16) for q in range(2)]
            deg = buf(nc, p, "degree", [P, T])
            place = buf(nc, p, "place", [P, T])
            for w in ("in", "out"):
                L = lists[w]
                key_f = k.dst_f if w == "in" else k.src_f
                split_keys(nc, k, key_f)
                histogram(nc, k, oh, deg)
                sort_by_degree(nc, k, deg, place, L.perm_d, L.keys_d, L.tiles_d, L.sched, L.perm, L.deg)
                with ExitStack() as q:
                    records = buf(nc, q, "records", [P, ECOL, REC])
                    empty = buf(nc, q, "empty", [P, 2 * S, REC])
                    fill_records(nc, k, records, empty, w)
                    prefill(nc, k, empty, L.list_d.rearrange("(h g p s) r -> h g p (s r)", p=P, s=S, g=2), L.sched)
                    place_edges(nc, k, key_f, oh, place, records, L.list_d)
        k.x = buf(nc, c, "x_rows", [P, T, P])
        k.h = buf(nc, c, "h_rows", [P, T, P])
        k.q = buf(nc, c, "q_rows", [P, T, P + 1])
        k.acc = buf(nc, c, "sums", [P, T, 16 * (D_HEAD + 1)])
        k.nm = buf(nc, c, "neg_max", [P, T, 16])
        k.perm1 = buf(nc, c, "perm1", [P, T], I32)
        k.eps = buf(nc, c, "eps", [P, 1])
        k.gate = buf(nc, c, "gate", [P, 2])
        k.w1 = buf(nc, c, "w1", [P, P])
        k.w2 = buf(nc, c, "w2", [P, P])
        k.b1 = buf(nc, c, "b1", [1, P])
        with nc.Block() as block:
            @block.vector
            def _(dve):
                dve.memset(k.eps[:], EPS)
        k.perm = lists["in"].perm
        L = lists["in"]
        listed = lambda L: (L.list_d.rearrange("(g p s) r -> g p (s r)", p=P, s=S), L.tiles_d.rearrange("(g b) -> g b", b=B), L.sched)
        load_nodes(nc, k, I["x"])
        load_weights(nc, k, [(k.w1[:], I["L0_gnn_Wn"]), (k.b1[:], row(I["L0_gnn_bn"]))])
        embed(nc, k)
        with ExitStack() as s:
            k.wz = buf(nc, s, "wz", [P, P + 1])
            k.bz = buf(nc, s, "bz", [1, P + 1])
            k.wvo = buf(nc, s, "wvo", [P, P])
            k.bvo = buf(nc, s, "bvo", [P, P])
            k.bo = buf(nc, s, "bo", [1, P])
            k.gb = buf(nc, s, "ln_g", [P, P])
            k.bb = buf(nc, s, "ln_b", [P, P])
            with nc.Fori(0, k.layers) as l:
                layer_weights(nc, k, I, l)
                project(nc, k)
                edge_pass(nc, k, "attend", k.table_d, NPAD, P, *listed(L))
                update(nc, k)
        load_weights(nc, k, [(k.w1[:], I["L0_gnn_Wout"]), (k.b1[:], row(I["L0_gnn_bout"]))])
        copy_out(nc, k)
        with ExitStack() as s:
            k.wkv = buf(nc, s, "wkv", [P, 4 * P])
            k.bkv = buf(nc, s, "bkv", [1, 4 * P])
            heads_weights(nc, k, I)
            heads_project(nc, k)
        edge_pass(nc, k, "heads", k.pairs_d, 2 * NPAD, 2 * P, *listed(L))
        gate_columns(nc, k, I["L1_gnn_skip"])
        load_weights(nc, k, [(k.w1[:], I["L1_gnn_Wa"]), (k.b1[:], row(I["L1_gnn_ba"]))])
        with ExitStack() as s:
            k.two = buf(nc, s, "two", [P, 2, GT, P])
            heads_out(nc, k)
        L = lists["out"]
        resort(nc, k, rows_d, L.perm)
        k.perm, k.deg_s = L.perm, L.deg
        k.inv = buf(nc, c, "inv_degree", [P, T])
        k.dis = buf(nc, c, "root_degree", [P, T])
        degree_columns(nc, k)
        norm_only(nc, k, k.h)
        load_weights(nc, k, [(k.w1[:], I["L2_gnn_W"][0:P]), (k.w2[:], I["L2_gnn_W"][P:2 * P]), (k.b1[:], row(I["L2_gnn_b"]))])
        edge_pass(nc, k, "weigh", k.table_d, NPAD, P, *listed(L))
        mean_out(nc, k)
        norm_only(nc, k, k.h, scale=k.dis)
        turn_weight(nc, k, I["L3_gnn_W"])
        load_weights(nc, k, [(k.b1[:], row(I["L3_gnn_b"]))])
        edge_pass(nc, k, "sum", k.table_d, NPAD, P, *listed(L))
        final_out(nc, k, out_d)


def fill_records(nc, k, records, empty, w):
    with ExitStack() as s:
        m = open_stage(nc, s, ["own"])
        t = buf(nc, s, "relation_1", [P, ECOL])
        with nc.Block() as block:
            @block.vector
            def _(dve):
                own = Steps(dve, m["own"])
                other = k.src_f if w == "in" else k.dst_f
                dve.tensor_copy(records[:, :, 0], other[:])
                dve.memset(records[:, :, 2], 0.0)
                dve.memset(empty[:, :, 0:2], float(PAD_ROW))
                dve.memset(empty[:, :, 2:3], -BIG)
                dve.memset(empty[:, :, 3:4], 2.0 if w == "in" else 0.0)
                if w == "in":
                    own(dve.tensor_scalar(t[:], k.kind_f[:], 0.0, float(NPAD), ALU.is_equal, ALU.mult))
                    own.wait()
                    dve.tensor_tensor(records[:, :, 1], t[:], other[:], ALU.add)
                    dve.tensor_copy(records[:, :, 3], k.kind_f[:])
                else:
                    dve.tensor_copy(records[:, :, 1], other[:])
                    dve.tensor_copy(records[:, :, 3], k.weight_f[:])
        close_stage(nc, m)


INPUTS = ["x", "src", "dst", "edge_type_2", "edge_weight1"] + [f"L0_gnn_{n}" for n in (
    "Wn", "bn", "WQ", "bQ", "WK", "bK", "WV", "bV", "WO", "bO", "ln_g", "ln_b", "Wout", "bout")] + [
    f"L1_gnn_{n}" for n in ("Wk", "bk", "Wq", "bq", "Wv", "bv", "a_rel", "m_rel", "p_rel", "Wa", "ba", "skip")] + [
    "L2_gnn_W", "L2_gnn_b", "L3_gnn_W", "L3_gnn_b"]


def kernel(**inputs):
    import concourse.bacc as bacc
    from concourse.bass_utils import run_bass_kernel_spmd

    nc = bacc.Bacc("TRN2", target_bir_lowering=False, num_devices=1)
    arrays, handles = {}, {}
    for name in INPUTS:
        a = np.ascontiguousarray(inputs[name])
        a = a.reshape(1) if a.ndim == 0 else a
        arrays[f"in_{name}"] = a
        handles[name] = nc.dram_tensor(f"in_{name}", a.shape, mybir.dt.from_np(a.dtype), kind="ExternalInput").ap()
    out = nc.dram_tensor("out_rows", [N, P], F32, kind="ExternalOutput").ap()
    gnn_kernel(nc, handles, out)
    return run_bass_kernel_spmd(nc, [arrays], core_ids=[0]).results[0]["out_rows"]
```
